# Optimizing a Trainium2 kernel written in Bass

```python
import numpy as np
import jax
import jax.numpy as jnp

def _softmax(x, axis=-1):
    return jax.nn.softmax(x, axis=axis)

def _gelu(x):
    return jax.nn.gelu(x, approximate=True)

def _silu(x):
    return jax.nn.silu(x)

def _sigmoid(x):
    return jax.nn.sigmoid(x)

def _layernorm(x, axis=-1, eps=1e-05):
    m = jnp.mean(x, axis=axis, keepdims=True)
    v = jnp.var(x, axis=axis, keepdims=True)
    return (x - m) / jnp.sqrt(v + eps)

def _scatter_add(tgt, idx, src, axis=0):
    return tgt.at[idx].add(src)

def _segment_sum(src, seg, n):
    return jax.ops.segment_sum(src, seg, n)
kernel_name = 'mk_seq_preln_d1_jaxref_r8_b95a69'

def setup_inputs(seed: int=0):
    np.random.seed(seed)
    _w = jnp.asarray

    def _L0_attn_setup():
        import jax, jax.numpy as jnp
        from jax import lax
        import numpy as np
        D_MODEL = 128
        D_STATE = 16
        D_CONV = 4
        EXPAND = 2
        D_INNER = EXPAND * D_MODEL
        DT_RANK = -(-D_MODEL // 16)
        BATCH, SEQLEN = (2, 128)

        def _mamba_block(x, ln_g, ln_b, W_in, conv_w, conv_b, W_xp, W_dt, b_dt, A_log, D_param, W_out, res_scale):
            B, L, D = x.shape
            E, N, K, R = (D_INNER, D_STATE, D_CONV, DT_RANK)
            mu = jnp.mean(x, axis=-1, keepdims=True)
            var = jnp.mean(jnp.square(x - mu), axis=-1, keepdims=True)
            xn = (x - mu) * lax.rsqrt(var + 1e-05) * ln_g + ln_b
            xz = jnp.einsum('bld,de->ble', xn, W_in)
            u, z = jnp.split(xz, 2, axis=-1)
            uc = u.transpose(0, 2, 1)
            conv = lax.conv_general_dilated(uc, conv_w[:, None, :], window_strides=(1,), padding=[(K - 1, 0)], feature_group_count=E, dimension_numbers=('NCH', 'OIH', 'NCH'))
            u2 = jax.nn.silu(conv + conv_b[None, :, None]).transpose(0, 2, 1)
            x_dbl = jnp.einsum('ble,er->blr', u2, W_xp)
            dt_lo, Bm, Cm = (x_dbl[..., :R], x_dbl[..., R:R + N], x_dbl[..., R + N:])
            dt = jax.nn.softplus(jnp.einsum('blr,re->ble', dt_lo, W_dt) + b_dt)
            A = -jnp.exp(A_log)

            def step(h, inp):
                dt_t, B_t, C_t, u_t = inp
                dA = jnp.exp(dt_t[..., None] * A)
                h = dA * h + (dt_t * u_t)[..., None] * B_t[:, None, :]
                y_t = jnp.einsum('ben,bn->be', h, C_t)
                return (h, y_t)
            h0 = jnp.zeros((B, E, N), x.dtype)
            xs = (dt.transpose(1, 0, 2), Bm.transpose(1, 0, 2), Cm.transpose(1, 0, 2), u2.transpose(1, 0, 2))
            _, ys = lax.scan(step, h0, xs)
            y = ys.transpose(1, 0, 2) + u2 * D_param
            y = y * jax.nn.silu(z)
            out = jnp.einsum('ble,ed->bld', y, W_out)
            return x + res_scale * out
        key = jax.random.key(seed)
        ks = jax.random.split(key, 12)
        s_in = 1.0 / np.sqrt(D_MODEL)
        s_e = 1.0 / np.sqrt(D_INNER)
        s_r = 1.0 / np.sqrt(DT_RANK)
        x = jax.random.normal(ks[0], (BATCH, SEQLEN, D_MODEL), jnp.float32)
        ln_g = jnp.ones((D_MODEL,), jnp.float32)
        ln_b = jnp.zeros((D_MODEL,), jnp.float32)
        W_in = jax.random.normal(ks[1], (D_MODEL, 2 * D_INNER), jnp.float32) * s_in
        conv_w = jax.random.normal(ks[2], (D_INNER, D_CONV), jnp.float32) * (1.0 / np.sqrt(D_CONV))
        conv_b = jnp.zeros((D_INNER,), jnp.float32)
        W_xp = jax.random.normal(ks[3], (D_INNER, DT_RANK + 2 * D_STATE), jnp.float32) * s_e
        W_dt = jax.random.normal(ks[4], (DT_RANK, D_INNER), jnp.float32) * s_r
        dt = jnp.exp(jax.random.uniform(ks[5], (D_INNER,)) * (np.log(0.1) - np.log(0.001)) + np.log(0.001))
        b_dt = dt + jnp.log(-jnp.expm1(-dt))
        A_log = jnp.log(jnp.broadcast_to(jnp.arange(1, D_STATE + 1, dtype=jnp.float32), (D_INNER, D_STATE)))
        D_param = jnp.ones((D_INNER,), jnp.float32)
        W_out = jax.random.normal(ks[6], (D_INNER, D_MODEL), jnp.float32) * s_e
        res_scale = jnp.ones((1,), jnp.float32)
        return dict(x=x, ln_g=ln_g, ln_b=ln_b, W_in=W_in, conv_w=conv_w, conv_b=conv_b, W_xp=W_xp, W_dt=W_dt, b_dt=b_dt, A_log=A_log, D_param=D_param, W_out=W_out, res_scale=res_scale)
    _L0_attn_in = _L0_attn_setup()

    def _L0_ffn_setup():
        import jax, jax.numpy as jnp
        import numpy as np
        E = 8
        TOPK = 2
        PRIME = 11
        HASH_OFF = 7919
        N_SHARED = 1
        key = jax.random.key(seed)
        ks = jax.random.split(key, 8)
        B, T, C, Hs, Hr = (4, 1024, 128, 256, 128)
        sc = lambda k, shape, fan: jax.random.normal(k, shape, jnp.float32) * fan ** (-0.5)
        return {'x': jax.random.normal(ks[0], (B, T, C), jnp.float32), 't_emb': jax.random.normal(ks[1], (B, C), jnp.float32), 'sw1': sc(ks[2], (C, Hs), C), 'sb1': jnp.zeros((Hs,), jnp.float32), 'sw3': sc(ks[3], (C, Hs), C), 'sb3': jnp.zeros((Hs,), jnp.float32), 'sw2': sc(ks[4], (Hs, C), Hs), 'sb2': jnp.zeros((C,), jnp.float32), 'w1': sc(ks[5], (E, C, Hr), C), 'b1': jnp.zeros((E, Hr), jnp.float32), 'w2': sc(ks[6], (E, Hr, C), Hr), 'b2': jnp.zeros((E, C), jnp.float32)}
    _L0_ffn_in = _L0_ffn_setup()
    _d = {'L0_attn_x': _L0_attn_in['x'], 'L0_attn_ln_g': _L0_attn_in['ln_g'], 'L0_attn_ln_b': _L0_attn_in['ln_b'], 'L0_attn_W_in': _L0_attn_in['W_in'], 'L0_attn_conv_w': _L0_attn_in['conv_w'], 'L0_attn_conv_b': _L0_attn_in['conv_b'], 'L0_attn_W_xp': _L0_attn_in['W_xp'], 'L0_attn_W_dt': _L0_attn_in['W_dt'], 'L0_attn_b_dt': _L0_attn_in['b_dt'], 'L0_attn_A_log': _L0_attn_in['A_log'], 'L0_attn_D_param': _L0_attn_in['D_param'], 'L0_attn_W_out': _L0_attn_in['W_out'], 'L0_attn_res_scale': _L0_attn_in['res_scale'], 'L0_ffn_t_emb': _L0_ffn_in['t_emb'], 'L0_ffn_sw1': _L0_ffn_in['sw1'], 'L0_ffn_sb1': _L0_ffn_in['sb1'], 'L0_ffn_sw3': _L0_ffn_in['sw3'], 'L0_ffn_sb3': _L0_ffn_in['sb3'], 'L0_ffn_sw2': _L0_ffn_in['sw2'], 'L0_ffn_sb2': _L0_ffn_in['sb2'], 'L0_ffn_w1': _L0_ffn_in['w1'], 'L0_ffn_b1': _L0_ffn_in['b1'], 'L0_ffn_w2': _L0_ffn_in['w2'], 'L0_ffn_b2': _L0_ffn_in['b2']}
    _x0 = _d['L0_attn_x']
    _d['L0_attn_x'] = jax.random.normal(jax.random.fold_in(jax.random.key(seed), 1), (4, 512, 128), dtype=_x0.dtype)
    del _x0
    return _d

def reference(L0_attn_x, L0_attn_ln_g, L0_attn_ln_b, L0_attn_W_in, L0_attn_conv_w, L0_attn_conv_b, L0_attn_W_xp, L0_attn_W_dt, L0_attn_b_dt, L0_attn_A_log, L0_attn_D_param, L0_attn_W_out, L0_attn_res_scale, L0_ffn_t_emb, L0_ffn_sw1, L0_ffn_sb1, L0_ffn_sw3, L0_ffn_sb3, L0_ffn_sw2, L0_ffn_sb2, L0_ffn_w1, L0_ffn_b1, L0_ffn_w2, L0_ffn_b2):

    def _L0_attn_ref(x, ln_g, ln_b, W_in, conv_w, conv_b, W_xp, W_dt, b_dt, A_log, D_param, W_out, res_scale):
        import jax, jax.numpy as jnp
        from jax import lax
        import numpy as np
        D_MODEL = 128
        D_STATE = 16
        D_CONV = 4
        EXPAND = 2
        D_INNER = EXPAND * D_MODEL
        DT_RANK = -(-D_MODEL // 16)
        BATCH, SEQLEN = (2, 128)

        def _mamba_block(x, ln_g, ln_b, W_in, conv_w, conv_b, W_xp, W_dt, b_dt, A_log, D_param, W_out, res_scale):
            B, L, D = x.shape
            E, N, K, R = (D_INNER, D_STATE, D_CONV, DT_RANK)
            mu = jnp.mean(x, axis=-1, keepdims=True)
            var = jnp.mean(jnp.square(x - mu), axis=-1, keepdims=True)
            xn = (x - mu) * lax.rsqrt(var + 1e-05) * ln_g + ln_b
            xz = jnp.einsum('bld,de->ble', xn, W_in)
            u, z = jnp.split(xz, 2, axis=-1)
            uc = u.transpose(0, 2, 1)
            conv = lax.conv_general_dilated(uc, conv_w[:, None, :], window_strides=(1,), padding=[(K - 1, 0)], feature_group_count=E, dimension_numbers=('NCH', 'OIH', 'NCH'))
            u2 = jax.nn.silu(conv + conv_b[None, :, None]).transpose(0, 2, 1)
            x_dbl = jnp.einsum('ble,er->blr', u2, W_xp)
            dt_lo, Bm, Cm = (x_dbl[..., :R], x_dbl[..., R:R + N], x_dbl[..., R + N:])
            dt = jax.nn.softplus(jnp.einsum('blr,re->ble', dt_lo, W_dt) + b_dt)
            A = -jnp.exp(A_log)

            def step(h, inp):
                dt_t, B_t, C_t, u_t = inp
                dA = jnp.exp(dt_t[..., None] * A)
                h = dA * h + (dt_t * u_t)[..., None] * B_t[:, None, :]
                y_t = jnp.einsum('ben,bn->be', h, C_t)
                return (h, y_t)
            h0 = jnp.zeros((B, E, N), x.dtype)
            xs = (dt.transpose(1, 0, 2), Bm.transpose(1, 0, 2), Cm.transpose(1, 0, 2), u2.transpose(1, 0, 2))
            _, ys = lax.scan(step, h0, xs)
            y = ys.transpose(1, 0, 2) + u2 * D_param
            y = y * jax.nn.silu(z)
            out = jnp.einsum('ble,ed->bld', y, W_out)
            return x + res_scale * out
        return _mamba_block(x, ln_g, ln_b, W_in, conv_w, conv_b, W_xp, W_dt, b_dt, A_log, D_param, W_out, res_scale)

    def _L0_ffn_ref(x, t_emb, sw1, sb1, sw3, sb3, sw2, sb2, w1, b1, w2, b2):
        import jax, jax.numpy as jnp
        import numpy as np
        E = 8
        TOPK = 2
        PRIME = 11
        HASH_OFF = 7919
        N_SHARED = 1
        B, T, C = x.shape
        N = B * T
        xf = x.reshape(N, C)
        shared = jax.nn.silu(xf @ sw1 + sb1) * (xf @ sw3 + sb3) @ sw2 + sb2
        tok = jnp.arange(N)
        out = jnp.zeros((N, C), x.dtype)
        for k in range(TOPK):
            exp_ids = (tok * PRIME + k * HASH_OFF) % E
            sort_idx = jnp.argsort(exp_ids)
            xs = xf[sort_idx].reshape(E, N // E, C)
            h = jax.nn.gelu(jnp.einsum('enc,ech->enh', xs, w1) + b1[:, None, :], approximate=False)
            y = jnp.einsum('enh,ehc->enc', h, w2) + b2[:, None, :]
            out = out.at[sort_idx].add(y.reshape(N, C))
        out = out / TOPK
        return ((shared + out) / (N_SHARED + 1)).reshape(B, T, C)
    x = L0_attn_x
    x = x + _L0_attn_ref(_layernorm(x, axis=-1), L0_attn_ln_g, L0_attn_ln_b, L0_attn_W_in, L0_attn_conv_w, L0_attn_conv_b, L0_attn_W_xp, L0_attn_W_dt, L0_attn_b_dt, L0_attn_A_log, L0_attn_D_param, L0_attn_W_out, L0_attn_res_scale)
    x = x + _L0_ffn_ref(_layernorm(x, axis=-1), L0_ffn_t_emb, L0_ffn_sw1, L0_ffn_sb1, L0_ffn_sw3, L0_ffn_sb3, L0_ffn_sw2, L0_ffn_sb2, L0_ffn_w1, L0_ffn_b1, L0_ffn_w2, L0_ffn_b2)
    return x

_drawn_inputs = setup_inputs


def setup_inputs(seed=0):
    import zlib

    import numpy as np

    out = dict(_drawn_inputs(seed))
    spreads = {'L0_attn_ln_g': (1.0, 0.2),
     'L0_attn_ln_b': (0.0, 0.1),
     'L0_attn_conv_b': (0.0, 0.401),
     'L0_attn_D_param': (1.0, 0.2),
     'L0_ffn_sb1': (0.0, 0.557),
     'L0_ffn_sb3': (0.0, 0.559),
     'L0_ffn_sb2': (0.0, 0.298),
     'L0_ffn_b1': (0.0, 0.706),
     'L0_ffn_b2': (0.0, 0.484)}
    factors = {}
    for name, (base, spread) in spreads.items():
        noise = np.random.default_rng([zlib.crc32(name.encode()), seed]).standard_normal(out[name].shape)
        drawn = base * np.exp(spread * noise) if base else spread * noise
        out[name] = jnp.asarray(drawn.astype(out[name].dtype))
    for name, factor in factors.items():
        out[name] = (out[name] * factor).astype(out[name].dtype)
    return out
```

```python
import concourse.bass as bass
from concourse import mybir
from contextlib import ExitStack

SEQS, T, D = 4, 512, 128
E, N, R, TAPS = 256, 16, 8, 4
HALF = 2
CH = T // 128
EXPERTS, CLASS = 8, T // 8
HID = 256
VECS = 2 + 5 * HALF + EXPERTS
EPS = 1e-5
KEEP = T + TAPS - 1
STATES = 2
RING = 6
AHEAD = 8

ROW_C, ROW_B, ROW_DT, ROWS, SPLIT = (0, 32, 64), 16, 96, 104, 96

PROJ_STEPS = ["ln1", "xn", "tr1", "u0", "u1", "z0", "z1", "xd", "dt"]
FFN_STEPS = ["y", "wo", "ln2", "xn2", "tr2", "s0", "s1", "g0", "g1", "eu0", "eu1", "fo", "bt"]
PROJ_AT = {0: ["ln1"], 1: ["xn"], 2: ["tr1"], 3: ["u0", "u1"], 5: ["z0", "z1"], 7: ["xd"], 9: ["dt"]}
FFN_AT = {0: ["y"], 2: ["wo"], 3: ["ln2"], 4: ["xn2", "tr2"], 6: ["s0", "s1"], 8: ["g0", "g1"],
          10: ["eu0"], 11: ["eu1"], 12: ["fo"], 14: ["bt"]}
BANKS_OF = {"tr1": 1, "u0": 1, "u1": 1, "z0": 1, "z1": 1, "xd": 1, "dt": 2, "wo": 1, "tr2": 1,
            "s0": 1, "s1": 1, "g0": 1, "g1": 1, "eu0": 1, "eu1": 1, "fo": 1, "bt": 1, "bias": 1, "cols": 1}


def order():
    yield ("cols", 0)
    for s in PROJ_STEPS:
        yield (s, 0)
    yield ("bias", 0)
    for b in range(SEQS):
        for n in range(N):
            yield ("unit", b, n)
            if b > 0:
                for s in FFN_AT.get(n, []):
                    yield (s, b - 1)
            if b < SEQS - 1:
                for s in PROJ_AT.get(n, []):
                    yield (s, b + 1)
    for s in FFN_STEPS:
        yield (s, SEQS - 1)


def bank_uses():
    uses, at = {}, 0
    for item in order():
        if item[0] in BANKS_OF:
            uses[item] = list(range(at, at + BANKS_OF[item[0]]))
            at += BANKS_OF[item[0]]
    return uses


def experts_of(j):
    return [(11 * j + 7919 * k) % EXPERTS for k in range(2)]


def classes_of(e):
    return [next(j for j in range(8) if experts_of(j)[k] == e) for k in range(2)]


def build(nc, x, ln_g, ln_b, W_in, conv_w, conv_b, W_xp, W_dt, b_dt, A_log, D_param, W_out, res_scale,
          sw1, sb1, sw3, sb3, sw2, sb2, w1, b1, w2, b2, route, out):
    f32, bf16 = mybir.dt.float32, mybir.dt.bfloat16
    ALU, ACT = mybir.AluOpType, mybir.ActivationFunctionType
    USES = bank_uses()
    b_scratch = nc.dram_tensor("b_scratch", (SEQS, N, T), f32, kind="Internal").ap()

    with ExitStack() as ctx:
        def sb(name, shape, dt=f32):
            return ctx.enter_context(nc.sbuf_tensor(name, shape, dt))

        def ps(name, shape):
            return ctx.enter_context(nc.psum_tensor(name, shape, f32))

        def sem(name):
            return ctx.enter_context(nc.semaphore(name))

        ident = sb("ident", [128, 128])
        csel = sb("csel", [SPLIT, N, 128], bf16)
        vec_rows, cols = sb("vec_rows", [VECS, 128]), sb("cols", [128, VECS])
        g_col, b_col = cols[:, 0:1], cols[:, 1:2]
        cb_col, dtb_col, d_col, sb1_col, sb3_col = (cols[:, 2 + 2 * i:4 + 2 * i] for i in range(5))
        b1_col = cols[:, 12:VECS]
        w_in = sb("w_in", [128, 2 * E])
        w_conv = sb("w_conv", [128, TAPS, E])
        xp_in = sb("xp_in", [128, HALF, R + 2 * N])
        w_xp = sb("w_xp", [128, HALF, ROWS])
        w_dt = sb("w_dt", [ROWS, E])
        a_log, a_exp, a_neg = sb("a_log", [128, HALF, N]), sb("a_exp", [128, HALF, N]), sb("a_neg", [128, HALF, N])
        w_out = sb("w_out", [128, HALF, D])
        rs_col = sb("rs_col", [128, 1])
        w_s1, w_s3, w_s2 = sb("w_s1", [128, HID]), sb("w_s3", [128, HID]), sb("w_s2", [128, HALF, D])
        w_e1, w_e2h = sb("w_e1", [128, EXPERTS, 128]), sb("w_e2h", [128, EXPERTS, 128])
        bias_rows, route_sb = sb("bias_rows", [EXPERTS + 1, D]), sb("route_sb", [EXPERTS + 1, CH, 128])
        bias_tok = sb("bias_tok", [128, CH, D])
        k_eps, k_mhalf, k_one, k_mone = (sb(n, [128, CH]) for n in ("k_eps", "k_mhalf", "k_one", "k_mone"))

        xin = sb("xin", [128, SEQS, CH, D])
        stat1, stat2 = sb("stat1", [128, SEQS, CH, 6]), sb("stat2", [128, SEQS, CH, 6])
        mv1, mv2 = sb("mv1", [128, SEQS, CH, 2]), sb("mv2", [128, SEQS, CH, 2])
        tiny = sb("tiny", [128, SEQS, 16, CH])
        xn = sb("xn", [128, CH, D])
        xres = sb("xres", [128, 2, CH, D])
        xnT = sb("xnT", [128, 2, KEEP])
        u2, gz = sb("u2", [128, 2, HALF, T]), sb("gz", [128, 2, HALF, T])
        small = sb("small", [ROWS, 2, T])
        cparts = sb("cparts", [SPLIT, 2, T], bf16)
        crest = sb("crest", [SPLIT, T])
        cmid = sb("cmid", [SPLIT, T], bf16)
        bexp, brelu, bln, bcor = (sb(n, [128, HALF, T]) for n in ("bexp", "brelu", "bln", "bcor"))
        dt, wdt = sb("dt", [128, 2, HALF, T]), sb("wdt", [128, 2, HALF, T])
        bbc = sb("bbc", [128, RING * STATES, T])
        drive = sb("drive", [128, 3, HALF, T])
        h = sb("h", [128, 2, HALF, T])
        hc = sb("hc", [128, 2, HALF, T])
        yd, yg = sb("yd", [128, HALF, T]), sb("yg", [128, HALF, T])
        taps = yd[:, :, :].rearrange("p h t -> p (h t)").rearrange("p (e k) -> p e k", k=TAPS)
        w_e2 = yg[:, :, :].rearrange("p h t -> p (h t)").rearrange("p (e c) -> p e c", e=EXPERTS)
        x1, x1b = sb("x1", [128, CH, D]), sb("x1b", [128, CH, D])
        xn2, xT = sb("xn2", [128, CH, D]), sb("xT", [128, T])
        hs1, hs = sb("hs1", [128, HALF, T]), sb("hs", [128, HALF, T])
        he = sb("he", [128, EXPERTS, 2 * CLASS])
        fo, res = sb("fo", [128, T]), sb("res", [128, 2, CH, D])

        decay = [ps(f"decay{i}", [128, T]) for i in range(3)]
        cbc = ps("cbc", [128, T])
        yacc = ps("yacc", [128, HALF, T])
        bank = [ps(f"bank{i}", [128, T]) for i in range(2)]

        x_in = [sem(f"x_in{b}") for b in range(SEQS)]
        in_vecs, in_w_in, in_w_mid, in_w_scan, in_w_ffn = (
            sem(n) for n in ("in_vecs", "in_w_in", "in_w_mid", "in_w_scan", "in_w_ffn"))
        const_ok, pad_ok, conv_ok, xpz_ok, xpw_ok = (sem(n) for n in ("const_ok", "pad_ok", "conv_ok", "xpz_ok", "xpw_ok"))
        a_ok, aneg_ok, e2h_ok, bias_ok, cols_ok = (sem(n) for n in ("a_ok", "aneg_ok", "e2h_ok", "bias_ok", "cols_ok"))
        stat1_ok, mv1_ok, fac1_ok, stat2_ok, mv2_ok, fac2_ok = (
            sem(n) for n in ("stat1_ok", "mv1_ok", "fac1_ok", "stat2_ok", "mv2_ok", "fac2_ok"))
        pool_chain = sem("pool_chain")
        xn_ok, xres_ok, xnT_ok, u2_ok, gz_ok = (sem(n) for n in ("xn_ok", "xres_ok", "xnT_ok", "u2_ok", "gz_ok"))
        small_ok, hi_ok, rest_ok, mid_ok, low_ok = (sem(n) for n in ("small_ok", "hi_ok", "rest_ok", "mid_ok", "low_ok"))
        b_out = sem("b_out")
        bbc_in = [sem(f"bbc_in{i}") for i in range(RING)]
        babs_ok, brelu_ok, bexp_ok, bln_ok = (sem(n) for n in ("babs_ok", "brelu_ok", "bexp_ok", "bln_ok"))
        bcor_ok, bcor2_ok, bsum_ok, dt_ok, wdt_ok = (sem(n) for n in ("bcor_ok", "bcor2_ok", "bsum_ok", "dt_ok", "wdt_ok"))
        filled = sem("filled")
        freed = [sem(f"freed{i}") for i in range(2)]
        decay_ok, drive_ok, scan_ok, hc_ok, cbc_ok, yacc_ok = (
            sem(n) for n in ("decay_ok", "drive_ok", "scan_ok", "hc_ok", "cbc_ok", "yacc_ok"))
        yd_ok, yg_ok, x1_ok, x1b_ok, xn2_ok, xT_ok = (sem(n) for n in ("yd_ok", "yg_ok", "x1_ok", "x1b_ok", "xn2_ok", "xT_ok"))
        hs1_ok, hs_ok, he_ok, fo_ok, res_ok = (sem(n) for n in ("hs1_ok", "hs_ok", "he_ok", "fo_ok", "res_ok"))
        stored = sem("stored")

        def tokens(v):
            return v.rearrange("(i c jj) d -> jj i c d", c=CH, jj=2)

        block = ctx.enter_context(nc.Block())

        @block.sync
        def _(sp):
            for b in range(SEQS):
                for jj in range(2):
                    sp.dma_start(xin[64 * jj:64 * jj + 64, b], tokens(x[b])[jj]).then_inc(x_in[b], 16)
                if b == 0:
                    sp.dma_start(w_in[:, :], W_in).then_inc(in_w_in, 16)
                    sp.dma_start(taps.rearrange("p e k -> p (e k)"),
                                 conv_w.rearrange("e k -> (e k)").partition_broadcast(128)).then_inc(in_w_in, 16)
            sp.dma_start(w_out[:, :, :], W_out.rearrange("(h p) d -> p h d", p=128)).then_inc(in_w_ffn, 16)
            sp.dma_start(w_s1[:, :], sw1).then_inc(in_w_ffn, 16)
            sp.dma_start(w_s3[:, :], sw3).then_inc(in_w_ffn, 16)
            sp.dma_start(w_s2[:, :, :], sw2.rearrange("(h p) d -> p h d", p=128)).then_inc(in_w_ffn, 16)
            sp.dma_start(w_e1[:, :, :], w1.rearrange("e c h -> c e h")).then_inc(in_w_ffn, 16)
            sp.dma_start(w_e2, w2.rearrange("e h c -> h e c")).then_inc(in_w_ffn, 16)
            sp.dma_start(rs_col[:, :], res_scale.partition_broadcast(128)).then_inc(in_w_ffn, 16)

            def load_b(g):
                b, n = divmod(g, N)
                if g >= RING * STATES:
                    sp.wait_ge(drive_ok, g + STATES - RING * STATES)
                at = g % (RING * STATES)
                sp.dma_start(bbc[:, at:at + STATES, :].rearrange("p n t -> p (n t)"),
                             b_scratch[b, n:n + STATES, :].rearrange("n t -> (n t)").partition_broadcast(128))\
                  .then_inc(bbc_in[g // STATES % RING], 16)

            for item in order():
                if item[0] == "unit":
                    g = N * item[1] + item[2] + AHEAD
                    if g % STATES == 0 and g < N * SEQS:
                        load_b(g)
                if item[0] == "xd":
                    b = item[1]
                    sp.wait_ge(small_ok, b + 1)
                    sp.dma_start(b_scratch[b], small[ROW_B:ROW_B + N, b % 2, :]).then_inc(b_out, 16)
                    sp.wait_ge(b_out, 16 * (b + 1))
                    if b == 0:
                        for g in range(0, AHEAD, STATES):
                            load_b(g)
                if item[0] == "bt":
                    b = item[1]
                    sp.wait_ge(res_ok, b + 1)
                    for jj in range(2):
                        sp.dma_start(tokens(out[b])[jj], res[64 * jj:64 * jj + 64, b % 2]).then_inc(stored, 16)
            sp.wait_ge(stored, 32 * SEQS)

        @block.gpsimd
        def _(pool):
            chain = [0]

            def link(ins):
                chain[0] += 1
                ins.then_inc(pool_chain, 1)
                pool.wait_ge(pool_chain, chain[0])

            pool.dma_start(xp_in[:, :, :], W_xp.rearrange("(h p) r -> p h r", p=128)).then_inc(in_w_mid, 16)
            pool.dma_start(w_dt[ROW_DT:ROWS, :], W_dt).then_inc(in_w_mid, 16)
            pool.dma_start(a_log[:, :, :], A_log.rearrange("(h p) n -> p h n", p=128)).then_inc(in_w_scan, 16)

            nc.gpsimd.memset(k_eps[:, :], EPS)
            nc.gpsimd.memset(k_mhalf[:, :], -0.5)
            nc.gpsimd.memset(k_one[:, :], 1.0)
            nc.gpsimd.memset(k_mone[:, :], -1.0)
            link(nc.gpsimd.memset(ident[:, :], 0.0))
            nc.gpsimd.affine_select(out=ident[:, :], in_=ident[:, :], compare_op=ALU.not_equal, fill=1.0, base=0,
                                    pattern=[[-1, 128]], channel_multiplier=1).then_inc(const_ok, 1)
            nc.gpsimd.memset(xnT[:, 0, 0:TAPS - 1], 0.0)
            nc.gpsimd.memset(xnT[:, 1, 0:TAPS - 1], 0.0).then_inc(pad_ok, 1)

            def factors(step, b, mv, k):
                f = [tiny[:, b, k + i, :] for i in range(8)]
                mean, var = mv[:, b, :, 0], mv[:, b, :, 1]
                tt = nc.gpsimd.tensor_tensor
                link(tt(out=f[0], in0=var, in1=k_eps[:, :], op=ALU.add))
                link(tt(out=f[1], in0=f[0], in1=k_mhalf[:, :], op=ALU.pow))
                link(tt(out=f[2], in0=mean, in1=k_mone[:, :], op=ALU.mult))
                return f

            def unit(g):
                b, n = divmod(g, N)
                if n == 0:
                    pool.wait_ge(wdt_ok, b + 1)
                if g % STATES == 0:
                    pool.wait_ge(bbc_in[g // STATES % RING], 16 * (g // STATES // RING + 1))
                if g >= 3:
                    pool.wait_ge(scan_ok, 2 * (g - 2))
                nc.gpsimd.tensor_tensor(out=drive[:, g % 3], in0=wdt[:, b % 2],
                                        in1=bbc[:, g % (RING * STATES), :].unsqueeze(1).broadcast_to([128, HALF, T]),
                                        op=ALU.mult).then_inc(drive_ok, 1)

            tt = nc.gpsimd.tensor_tensor
            for item in order():
                if item[0] == "bias":
                    link(nc.gpsimd.memset(csel[:, :, :], 0.0))
                    for q in ROW_C:
                        ins = nc.gpsimd.affine_select(out=csel[:, :, :], in_=csel[:, :, :], compare_op=ALU.not_equal,
                                                      fill=1.0, base=-q, pattern=[[-1, N], [0, 128]],
                                                      channel_multiplier=1)
                        if q == ROW_C[-1]:
                            ins.then_inc(const_ok, 1)
                        else:
                            link(ins)
                elif item[0] == "unit":
                    g = N * item[1] + item[2]
                    if g == 0:
                        unit(0)
                    if item[2] < N - 1:
                        unit(g + 1)
                elif item[0] == "ln1":
                    b = item[1]
                    pool.wait_ge(mv1_ok, CH * (b + 1))
                    f = factors("ln1", b, mv1, 0)
                    link(tt(out=f[3], in0=f[1], in1=f[1], op=ALU.mult))
                    link(tt(out=f[4], in0=f[3], in1=mv1[:, b, :, 1], op=ALU.mult))
                    link(tt(out=f[5], in0=f[4], in1=k_eps[:, :], op=ALU.add))
                    link(tt(out=f[6], in0=f[5], in1=k_mhalf[:, :], op=ALU.pow))
                    link(tt(out=f[7], in0=f[6], in1=f[1], op=ALU.mult))
                    tt(out=tiny[:, b, 12, :], in0=f[7], in1=f[2], op=ALU.mult)
                    tt(out=tiny[:, b, 13, :], in0=f[1], in1=k_one[:, :], op=ALU.add)
                    tt(out=tiny[:, b, 14, :], in0=f[1], in1=f[2], op=ALU.mult).then_inc(fac1_ok, 1)
                elif item[0] == "ln2":
                    b = item[1]
                    pool.wait_ge(mv2_ok, CH * (b + 1))
                    f = factors("ln2", b, mv2, 8)
                    tt(out=f[3], in0=f[1], in1=f[2], op=ALU.mult).then_inc(fac2_ok, 1)
                    if b == 0:
                        pool.wait_ge(bias_ok, 1)
                    if b >= 1:
                        pool.wait_ge(res_ok, b)
                    tt(out=x1b[:, :, :], in0=x1[:, :, :], in1=bias_tok[:, :, :], op=ALU.add).then_inc(x1b_ok, 1)
                elif item[0] == "xd":
                    b = item[1]
                    pool.wait_ge(hi_ok, b + 1)
                    tt(out=crest[:, :], in0=small[0:SPLIT, b % 2], in1=cparts[:, b % 2],
                       op=ALU.subtract).then_inc(rest_ok, 1)
                    pool.wait_ge(rest_ok, b + 1)
                    pool.wait_ge(mid_ok, 2 * (b + 1))
                    tt(out=cparts[64:96, b % 2], in0=crest[64:96, :], in1=cmid[64:96, :],
                       op=ALU.subtract).then_inc(low_ok, 1)
                    pool.wait_ge(low_ok, b + 1)
                elif item[0] == "dt":
                    b = item[1]
                    pool.wait_ge(bln_ok, b + 1)
                    pool.wait_ge(brelu_ok, 2 * (b + 1))
                    tt(out=bln[:, :, :], in0=bln[:, :, :], in1=brelu[:, :, :], op=ALU.add).then_inc(bsum_ok, 1)
                    pool.wait_ge(bcor2_ok, b + 1)
                    pool.wait_ge(bsum_ok, b + 1)
                    tt(out=dt[:, b % 2], in0=bln[:, :, :], in1=bcor[:, :, :], op=ALU.add).then_inc(dt_ok, 1)
                    pool.wait_ge(dt_ok, b + 1)
                    tt(out=wdt[:, b % 2], in0=dt[:, b % 2], in1=u2[:, b % 2], op=ALU.mult).then_inc(wdt_ok, 1)
                elif item[0] == "y":
                    b = item[1]
                    pool.wait_ge(yd_ok, 2 * (b + 1))
                    if b >= 1:
                        pool.wait_ge(x1_ok, b)
                    tt(out=yg[:, :, :].rearrange("p h (j i) -> p h j i", i=CLASS),
                       in0=yd[:, :, :].rearrange("p h (i j) -> p h j i", i=CLASS),
                       in1=gz[:, b % 2].rearrange("p h (i j) -> p h j i", i=CLASS), op=ALU.mult).then_inc(yg_ok, 1)
                if item[0] == "unit" and item[2] == N - 1 and item[1] < SEQS - 1:
                    unit(N * (item[1] + 1))

        @block.scalar
        def _(act):
            fn = nc.scalar.activation
            for i, vec in enumerate((ln_g, ln_b, conv_b, b_dt, D_param, sb1, sb3, b1)):
                row = i if i < 2 else 2 * i - 2
                src = vec if len(vec.shape) == 2 else vec.rearrange("(h p) -> h p", p=128)
                act.dma_start(vec_rows[row:row + src.shape[0], :], src).then_inc(in_vecs, 16)
            act.dma_start(bias_rows[0:EXPERTS, :], b2).then_inc(in_w_ffn, 16)
            act.dma_start(bias_rows[EXPERTS:EXPERTS + 1, :], sb2.rearrange("(o d) -> o d", o=1)).then_inc(in_w_ffn, 16)
            act.dma_start(route_sb[:, :, :], route).then_inc(in_w_ffn, 16)

            def full(item, k=0):
                u = USES[item][k]
                act.wait_ge(filled, u + 1)
                return bank[u % 2], u % 2

            def decays(g):
                b, n = divmod(g, N)
                if n == 0:
                    act.wait_ge(dt_ok, b + 1)
                    nc.scalar.preload_act_table_set("natural_log_exp_and_others")
                for hf in range(HALF):
                    r = 2 * g + hf
                    if r >= 3:
                        act.wait_ge(scan_ok, r - 2)
                    fn(decay[r % 3][:, :], dt[:, b % 2, hf, :], ACT.Exp,
                       scale=a_neg[:, hf, n:n + 1]).then_inc(decay_ok, 1)

            def log_exp():
                nc.scalar.preload_act_table_set("natural_log_exp_and_others")

            for item in order():
                s, b = item[0], item[1]
                if s == "unit":
                    g = N * b + item[2]
                    if g == 0:
                        act.wait_ge(aneg_ok, 1)
                        decays(0)
                    if g + 1 < N * SEQS:
                        decays(g + 1)
                elif s == "cols":
                    act.wait_ge(in_w_scan, 16)
                    fn(a_exp[:, :, :], a_log[:, :, :], ACT.Exp).then_inc(a_ok, 1)
                elif s == "xn":
                    act.wait_ge(fac1_ok, b + 1)
                    for c in range(CH):
                        ins = fn(xn[:, c, :], xin[:, b, c, :], ACT.Identity,
                                 scale=tiny[:, b, 7, c:c + 1], bias=tiny[:, b, 12, c:c + 1])
                    ins.then_inc(xn_ok, 1)
                elif s == "tr1":
                    m, k = full(item)
                    if b == 0:
                        act.wait_ge(cols_ok, 1)
                    fn(xnT[:, b % 2, TAPS - 1:].rearrange("p (i j) -> p j i", i=CLASS),
                       m[:, :].rearrange("p (j i) -> p j i", i=CLASS), ACT.Identity,
                       scale=g_col[:, :], bias=b_col[:, :]).then_inc(xnT_ok, 1)
                    act.wait_ge(xnT_ok, b + 1)
                    act.sem_inc(freed[k], 1)
                elif s in ("u0", "u1"):
                    m, k = full(item)
                    hf = int(s[1])
                    if b >= 2:
                        act.wait_ge(yd_ok, 2 * (b - 1))
                    fn(u2[:, b % 2, hf], m[:, :], ACT.Silu, bias=cb_col[:, hf:hf + 1]).then_inc(u2_ok, 1)
                    act.wait_ge(u2_ok, 2 * b + hf + 1)
                    act.sem_inc(freed[k], 1)
                elif s in ("z0", "z1"):
                    m, k = full(item)
                    hf = int(s[1])
                    if b >= 2:
                        act.wait_ge(yg_ok, b - 1)
                    fn(gz[:, b % 2, hf], m[:, :], ACT.Silu).then_inc(freed[k], 1)
                elif s == "xd":
                    m, k = full(item)
                    fn(small[:, b % 2], m[0:ROWS, :], ACT.Identity).then_inc(small_ok, 1)
                    act.wait_ge(small_ok, b + 1)
                    act.sem_inc(freed[k], 1)
                    fn(cparts[:, b % 2], small[0:SPLIT, b % 2], ACT.Identity).then_inc(hi_ok, 1)
                    act.wait_ge(rest_ok, b + 1)
                    fn(cparts[32:64, b % 2], crest[32:64, :], ACT.Identity).then_inc(mid_ok, 1)
                    fn(cmid[64:96, :], crest[64:96, :], ACT.Identity).then_inc(mid_ok, 1)
                    if b >= 2:
                        act.wait_ge(x1_ok, b - 1)
                    for c in range(CH):
                        ins = fn(xres[:, b % 2, c, :], xin[:, b, c, :], ACT.Identity,
                                 scale=tiny[:, b, 13, c:c + 1], bias=tiny[:, b, 14, c:c + 1])
                    ins.then_inc(xres_ok, 1)
                elif s == "dt":
                    log_exp()
                    for hf in range(HALF):
                        m, k = full(item, hf)
                        if b >= 1:
                            act.wait_ge(bcor2_ok, b)
                            act.wait_ge(dt_ok, b)
                        fn(bexp[:, hf], m[:, :], ACT.Abs, bias=dtb_col[:, hf:hf + 1]).then_inc(babs_ok, 1)
                        fn(brelu[:, hf], m[:, :], ACT.Relu, bias=dtb_col[:, hf:hf + 1]).then_inc(brelu_ok, 1)
                        act.wait_ge(brelu_ok, 2 * b + hf + 1)
                        act.sem_inc(freed[k], 1)
                    act.wait_ge(babs_ok, 2 * (b + 1))
                    fn(bexp[:, :, :], bexp[:, :, :], ACT.Exp, scale=-1.0).then_inc(bexp_ok, 1)
                    act.wait_ge(bexp_ok, b + 1)
                    fn(bln[:, :, :], bexp[:, :, :], ACT.Ln, bias=1.0).then_inc(bln_ok, 1)
                elif s == "xn2":
                    act.wait_ge(fac2_ok, b + 1)
                    if b >= 1:
                        act.wait_ge(xT_ok, b)
                    for c in range(CH):
                        ins = fn(xn2[:, c, :], x1[:, c, :], ACT.Identity,
                                 scale=tiny[:, b, 9, c:c + 1], bias=tiny[:, b, 11, c:c + 1])
                    ins.then_inc(xn2_ok, 1)
                elif s == "tr2":
                    m, k = full(item)
                    fn(xT[:, :], m[:, :], ACT.Identity).then_inc(xT_ok, 1)
                    act.wait_ge(xT_ok, b + 1)
                    act.sem_inc(freed[k], 1)
                elif s in ("s0", "s1"):
                    m, k = full(item)
                    hf = int(s[1])
                    fn(hs1[:, hf], m[:, :], ACT.Silu, bias=sb1_col[:, hf:hf + 1]).then_inc(hs1_ok, 1)
                    act.wait_ge(hs1_ok, 2 * b + hf + 1)
                    act.sem_inc(freed[k], 1)
                elif s in ("eu0", "eu1"):
                    m, k = full(item)
                    for i in range(4):
                        e = 4 * int(s[2]) + i
                        ins = fn(he[:, e, :], m[:, i * 128:(i + 1) * 128], ACT.Gelu, bias=b1_col[:, e:e + 1])
                    ins.then_inc(he_ok, 1)
                    act.wait_ge(he_ok, 2 * b + int(s[2]) + 1)
                    act.sem_inc(freed[k], 1)
                elif s == "fo":
                    m, k = full(item)
                    fn(fo[:, :], m[:, :], ACT.Identity).then_inc(fo_ok, 1)
                    act.wait_ge(fo_ok, b + 1)
                    act.sem_inc(freed[k], 1)

        @block.tensor
        def _(pe):
            mm = nc.tensor.matmul

            def take(item, k=0):
                u = USES[item][k]
                if u >= 2:
                    pe.wait_ge(freed[u % 2], u // 2)
                return bank[u % 2]

            def accumulate(g):
                b, n = divmod(g, N)
                pe.wait_ge(hc_ok, g + 1)
                if n == 0 and b >= 1:
                    pe.wait_ge(yd_ok, 2 * b)
                for hf in range(HALF):
                    ins = mm(yacc[:, hf, :], ident[:, :], hc[:, g % 2, hf], start=(n == 0), stop=(n == N - 1))
                ins.then_inc(yacc_ok, 1)

            for item in order():
                s, b = item[0], item[1]
                if s == "unit":
                    n = item[2]
                    g = N * b + n
                    if n == 0:
                        if b == 0:
                            pe.wait_ge(const_ok, 2)
                        pe.wait_ge(low_ok, b + 1)
                        pe.wait_ge(mid_ok, 2 * (b + 1))
                    if g >= 1:
                        pe.wait_ge(hc_ok, g)
                    mm(cbc[:, :], csel[:, n, :], cparts[:, b % 2], start=True, stop=True).then_inc(cbc_ok, 1)
                    if n >= 1:
                        accumulate(g - 1)
                elif s == "cols":
                    pe.wait_ge(const_ok, 1)
                    pe.wait_ge(in_vecs, 16 * 8)
                    nc.tensor.transpose(take(item)[:, 0:VECS], vec_rows[:, :], ident[0:VECS, 0:VECS]).then_inc(filled, 1)
                elif s == "bias":
                    pe.wait_ge(in_w_ffn, 16 * 10)
                    m = take(item)
                    for c in range(CH):
                        ins = mm(m[:, c * D:(c + 1) * D], route_sb[:, c, :], bias_rows[:, :], start=True, stop=True)
                    ins.then_inc(filled, 1)
                elif s == "tr1":
                    m = take(item)
                    if b == 0:
                        pe.wait_ge(const_ok, 1)
                    pe.wait_ge(xn_ok, b + 1)
                    for c in range(CH):
                        ins = nc.tensor.transpose(m[:, c * 128:(c + 1) * 128], xn[:, c, :], ident[:, :])
                    ins.then_inc(filled, 1)
                elif s in ("u0", "u1"):
                    m = take(item)
                    hf = int(s[1])
                    if b == 0 and hf == 0:
                        pe.wait_ge(conv_ok, 1)
                        pe.wait_ge(pad_ok, 1)
                    pe.wait_ge(xnT_ok, b + 1)
                    for k in range(TAPS):
                        ins = mm(m[:, :], w_conv[:, k, hf * 128:(hf + 1) * 128], xnT[:, b % 2, k:k + T],
                                 start=(k == 0), stop=(k == TAPS - 1))
                    ins.then_inc(filled, 1)
                elif s in ("z0", "z1"):
                    m = take(item)
                    hf = int(s[1])
                    mm(m[:, :], w_in[:, E + hf * 128:E + (hf + 1) * 128], xnT[:, b % 2, TAPS - 1:],
                       start=True, stop=True).then_inc(filled, 1)
                elif s == "xd":
                    m = take(item)
                    if b == 0:
                        pe.wait_ge(xpw_ok, 9 + 1)
                    pe.wait_ge(u2_ok, 2 * (b + 1))
                    for hf in range(HALF):
                        ins = mm(m[0:ROWS, :], w_xp[:, hf, :], u2[:, b % 2, hf], start=(hf == 0), stop=(hf == 1))
                    ins.then_inc(filled, 1)
                elif s == "dt":
                    pe.wait_ge(small_ok, b + 1)
                    for hf in range(HALF):
                        m = take(item, hf)
                        mm(m[:, :], w_dt[ROW_DT:ROWS, hf * 128:(hf + 1) * 128], small[ROW_DT:ROWS, b % 2],
                           start=True, stop=True).then_inc(filled, 1)
                elif s == "y":
                    accumulate(N * b + N - 1)
                elif s == "wo":
                    m = take(item)
                    pe.wait_ge(yg_ok, b + 1)
                    for c in range(CH):
                        for hf in range(HALF):
                            ins = mm(m[:, c * D:(c + 1) * D], yg[:, hf, c * 128:(c + 1) * 128], w_out[:, hf, :],
                                     start=(hf == 0), stop=(hf == 1))
                    ins.then_inc(filled, 1)
                elif s == "tr2":
                    m = take(item)
                    pe.wait_ge(xn2_ok, b + 1)
                    for c in range(CH):
                        ins = nc.tensor.transpose(m[:, c * 128:(c + 1) * 128], xn2[:, c, :], ident[:, :])
                    ins.then_inc(filled, 1)
                elif s in ("s0", "s1", "g0", "g1"):
                    m = take(item)
                    hf = int(s[1])
                    pe.wait_ge(xT_ok, b + 1)
                    w = w_s1 if s[0] == "s" else w_s3
                    mm(m[:, :], w[:, hf * 128:(hf + 1) * 128], xT[:, :], start=True, stop=True).then_inc(filled, 1)
                elif s in ("eu0", "eu1"):
                    m = take(item)
                    for i in range(4):
                        e = 4 * int(s[2]) + i
                        for k, j in enumerate(classes_of(e)):
                            ins = mm(m[:, i * 128 + k * CLASS:i * 128 + (k + 1) * CLASS], w_e1[:, e, :],
                                     xT[:, j * CLASS:(j + 1) * CLASS], start=True, stop=True)
                    ins.then_inc(filled, 1)
                elif s == "fo":
                    m = take(item)
                    pe.wait_ge(hs_ok, 2 * (b + 1))
                    mm(m[:, :], w_s2[:, 0, :], hs[:, 0], start=True, stop=False)
                    pe.wait_ge(he_ok, 2 * (b + 1))
                    if b == 0:
                        pe.wait_ge(e2h_ok, 1)
                    for e in range(EXPERTS):
                        for k, j in enumerate(classes_of(e)):
                            mm(m[:, j * CLASS:(j + 1) * CLASS], w_e2h[:, e, :],
                                     he[:, e, k * CLASS:(k + 1) * CLASS], start=False, stop=False)
                    mm(m[:, :], w_s2[:, 1, :], hs[:, 1], start=False, stop=True).then_inc(filled, 1)
                elif s == "bt":
                    m = take(item)
                    pe.wait_ge(fo_ok, b + 1)
                    for c in range(CH):
                        ins = nc.tensor.transpose(m[:, c * 128:(c + 1) * 128], fo[:, c * 128:(c + 1) * 128], ident[:, :])
                    ins.then_inc(filled, 1)

        @block.vector
        def _(dve):
            v = nc.vector

            def full(item, k=0):
                u = USES[item][k]
                dve.wait_ge(filled, u + 1)
                return bank[u % 2], u % 2

            def stats(src, stat, mv, stat_ok, mv_ok, b):
                for c in range(CH):
                    v.bn_stats(out=stat[:, b, c, :], in_=src[:, c, :]).then_inc(stat_ok, 1)
                for c in range(CH):
                    dve.wait_ge(stat_ok, CH * b + c + 1)
                    v.bn_aggr(out=mv[:, b, c, :], in_=stat[:, b, c, :]).then_inc(mv_ok, 1)

            v.memset(w_xp[:, :, :], 0.0).then_inc(xpz_ok, 1)

            for item in order():
                s, b = item[0], item[1]
                if s == "unit":
                    n = item[2]
                    g = N * b + n
                    dve.wait_ge(drive_ok, g + 1)
                    for hf in range(HALF):
                        r = 2 * g + hf
                        dve.wait_ge(decay_ok, r + 1)
                        v.tensor_tensor_scan(h[:, g % 2, hf, :], decay[r % 3][:, :], drive[:, g % 3, hf], 0.0,
                                             ALU.mult, ALU.add).then_inc(scan_ok, 1)
                    dve.wait_ge(scan_ok, 2 * g + 2)
                    dve.wait_ge(cbc_ok, g + 1)
                    if g >= 2:
                        dve.wait_ge(yacc_ok, g - 1)
                    v.tensor_tensor(out=hc[:, g % 2], in0=h[:, g % 2],
                                    in1=cbc[:, :].unsqueeze(1).broadcast_to([128, HALF, T]),
                                    op=ALU.mult).then_inc(hc_ok, 1)
                elif s == "ln1":
                    dve.wait_ge(x_in[b], 32)
                    stats(xin[:, b], stat1, mv1, stat1_ok, mv1_ok, b)
                    if b == 0:
                        dve.wait_ge(in_w_in, 32)
                        for k in range(TAPS):
                            ins = v.tensor_tensor(out=w_conv[:, k, :], in0=w_in[:, 0:E], in1=taps[:, :, k], op=ALU.mult)
                        ins.then_inc(conv_ok, 1)
                        dve.wait_ge(in_w_mid, 32)
                        dve.wait_ge(xpz_ok, 1)
                        for hf in range(HALF):
                            for q in ROW_C:
                                v.tensor_copy(w_xp[:, hf, q:q + N], xp_in[:, hf, R + N:R + 2 * N]).then_inc(xpw_ok, 1)
                            v.tensor_copy(w_xp[:, hf, ROW_B:ROW_B + N], xp_in[:, hf, R:R + N]).then_inc(xpw_ok, 1)
                            v.tensor_copy(w_xp[:, hf, ROW_DT:ROWS], xp_in[:, hf, 0:R]).then_inc(xpw_ok, 1)
                        dve.wait_ge(a_ok, 1)
                        v.tensor_scalar(a_neg[:, :, :], a_exp[:, :, :], -1.0, None, ALU.mult).then_inc(aneg_ok, 1)
                elif s == "cols":
                    m, k = full(item)
                    v.tensor_copy(cols[:, :], m[:, 0:VECS]).then_inc(cols_ok, 1)
                    dve.wait_ge(cols_ok, 1)
                    dve.sem_inc(freed[k], 1)
                elif s == "bias":
                    m, k = full(item)
                    v.tensor_copy(bias_tok[:, :, :].rearrange("p c d -> p (c d)"), m[:, :]).then_inc(bias_ok, 1)
                    dve.wait_ge(bias_ok, 1)
                    dve.sem_inc(freed[k], 1)
                    v.tensor_scalar(w_e2h[:, :, :], w_e2, 0.5, None, ALU.mult).then_inc(e2h_ok, 1)
                elif s == "dt":
                    dve.wait_ge(bexp_ok, b + 1)
                    if b >= 1:
                        dve.wait_ge(dt_ok, b)
                    v.tensor_scalar(bcor[:, :, :], bexp[:, :, :], 1.0, 1.0, ALU.add, ALU.subtract).then_inc(bcor_ok, 1)
                    dve.wait_ge(bcor_ok, b + 1)
                    v.tensor_tensor(out=bcor[:, :, :], in0=bexp[:, :, :], in1=bcor[:, :, :],
                                    op=ALU.subtract).then_inc(bcor2_ok, 1)
                elif s == "y":
                    dve.wait_ge(yacc_ok, N * (b + 1))
                    if b >= 1:
                        dve.wait_ge(yg_ok, b)
                    for hf in range(HALF):
                        v.scalar_tensor_tensor(out=yd[:, hf], in0=u2[:, b % 2, hf], scalar=d_col[:, hf:hf + 1],
                                               in1=yacc[:, hf, :], op0=ALU.mult, op1=ALU.add).then_inc(yd_ok, 1)
                elif s == "wo":
                    m, k = full(item)
                    dve.wait_ge(xres_ok, b + 1)
                    if b >= 1:
                        dve.wait_ge(xn2_ok, b)
                        dve.wait_ge(x1b_ok, b)
                    v.scalar_tensor_tensor(out=x1[:, :, :].rearrange("p c d -> p (c d)"), in0=m[:, :], scalar=rs_col[:, :],
                                           in1=xres[:, b % 2].rearrange("p c d -> p (c d)"),
                                           op0=ALU.mult, op1=ALU.add).then_inc(x1_ok, 1)
                    dve.wait_ge(x1_ok, b + 1)
                    dve.sem_inc(freed[k], 1)
                elif s == "ln2":
                    stats(x1, stat2, mv2, stat2_ok, mv2_ok, b)
                elif s in ("g0", "g1"):
                    m, k = full(item)
                    hf = int(s[1])
                    dve.wait_ge(hs1_ok, 2 * b + hf + 1)
                    v.scalar_tensor_tensor(out=hs[:, hf], in0=m[:, :], scalar=sb3_col[:, hf:hf + 1], in1=hs1[:, hf],
                                           op0=ALU.add, op1=ALU.mult).then_inc(hs_ok, 1)
                    dve.wait_ge(hs_ok, 2 * b + hf + 1)
                    dve.sem_inc(freed[k], 1)
                elif s == "bt":
                    m, k = full(item)
                    dve.wait_ge(x1b_ok, b + 1)
                    if b >= 2:
                        dve.wait_ge(stored, 32 * (b - 1))
                    v.scalar_tensor_tensor(out=res[:, b % 2].rearrange("p c d -> p (c d)"), in0=m[:, :], scalar=0.5,
                                           in1=x1b[:, :, :].rearrange("p c d -> p (c d)"),
                                           op0=ALU.mult, op1=ALU.add).then_inc(res_ok, 1)
                    dve.wait_ge(res_ok, b + 1)
                    dve.sem_inc(freed[k], 1)


_INS = ['L0_attn_x', 'L0_attn_ln_g', 'L0_attn_ln_b', 'L0_attn_W_in', 'L0_attn_conv_w', 'L0_attn_conv_b',
        'L0_attn_W_xp', 'L0_attn_W_dt', 'L0_attn_b_dt', 'L0_attn_A_log', 'L0_attn_D_param', 'L0_attn_W_out',
        'L0_attn_res_scale', 'L0_ffn_sw1', 'L0_ffn_sb1', 'L0_ffn_sw3', 'L0_ffn_sb3', 'L0_ffn_sw2', 'L0_ffn_sb2',
        'L0_ffn_w1', 'L0_ffn_b1', 'L0_ffn_w2', 'L0_ffn_b2']


def kernel(**inputs):
    import numpy as _np
    import concourse.bacc as _bacc
    from concourse import mybir as _mybir
    from concourse.bass_utils import run_bass_kernel_spmd as _run

    nc = _bacc.Bacc("TRN2", target_bir_lowering=False, num_devices=1)
    arrays, args = {}, []
    for name in _INS:
        a = _np.ascontiguousarray(inputs[name])
        arrays[f"in_{name}_dram"] = a
        args.append(nc.dram_tensor(f"in_{name}_dram", a.shape, _mybir.dt.from_np(a.dtype), kind="ExternalInput").ap())
    route = _np.zeros((EXPERTS + 1, CH, 128), _np.float32)
    for j in range(8):
        at = slice(64 * (j % 2), 64 * (j % 2) + 64)
        for e in experts_of(j):
            route[e, j // 2, at] = 0.25
        route[EXPERTS, j // 2, at] = 0.5
    arrays["route_dram"] = route
    args.append(nc.dram_tensor("route_dram", route.shape, _mybir.dt.float32, kind="ExternalInput").ap())
    args.append(nc.dram_tensor("out_0_dram", (SEQS, T, D), _mybir.dt.float32, kind="ExternalOutput").ap())
    build(nc, *args)
    r = _run(nc, [arrays], core_ids=[0])
    return r.results[0]["out_0_dram"]
```

```python
import concourse.bass as bass
from concourse import mybir
from contextlib import ExitStack

SEQS, T, D = 4, 512, 128
E, N, R, TAPS = 256, 16, 8, 4
HALF = 2
CH = T // 128
EXPERTS, CLASS = 8, T // 8
HID = 256
VECS = 2 + 5 * HALF + EXPERTS
VECS1 = 2 + 2 * HALF
EPS = 1e-5
KEEP = T + TAPS - 1
STATES = 2
RING = 6
WARM = 16
AHEAD = 8

ROW_C, ROW_B, ROW_DT, ROWS, SPLIT = (0, 32, 64), 16, 96, 104, 96

FIRST = {
    "PE": [("warm", 0), ("cols", 0), ("tr1", 0), ("u0a", 0), ("u0b", 0), ("u1a", 0), ("u1b", 0), ("xd", 0), ("dt", 0),
           ("tr1", 1), ("z0", 0), ("z1", 0), ("tr1", 2), ("tr1", 3), ("cols2", 0), ("bias", 0)],
    "ACT": [("cols", 0), ("xn", 0), ("tr1", 0), ("u0", 0), ("xn", 1), ("u1", 0), ("xd", 0), ("relu", 0), ("exp", 0),
            ("ln", 0), ("mid", 0), ("tr1", 1), ("z0", 0), ("z1", 0), ("tr1", 2), ("tr1", 3)],
    "DVE": [("ln1", 0), ("weights", 0), ("cols", 0), ("ln1", 1), ("ln1", 2), ("ln1", 3), ("csel", 0), ("xres", 0),
            ("xres", 1), ("xres", 2), ("xres", 3), ("cor", 0), ("sum", 0), ("dt", 0), ("wdt", 0), ("cols2", 0),
            ("bias", 0)],
    "POOL": [("fac1", 0), ("csel", 0), ("fac1", 1), ("rest", 0), ("low", 0)],
    "SP": [("b_out", 0)],
}
PROJ = {
    "PE": {0: ["u0a"], 1: ["u0b"], 2: ["u1a"], 3: ["u1b"], 5: ["z0", "z1"], 6: ["xd"], 7: ["dt"]},
    "ACT": {4: ["u0", "u1"], 6: ["z0", "z1"], 7: ["xd"], 8: ["relu", "exp"], 9: ["ln", "mid"]},
    "DVE": {9: ["cor"]},
    "POOL": {8: ["rest"], 10: ["sum"], 11: ["dt"], 12: ["wdt"], 13: ["low"]},
    "SP": {7: ["b_out"]},
}
FFN = {
    "PE": {0: ["y"], 4: ["wo"], 8: ["tr2"], 10: ["s0", "s1"], 11: ["g0", "g1"], 12: ["eu0", "eu1"], 13: ["fo0"],
           14: ["fo1"], 15: ["fo2"], 20: ["bt"]},
    "ACT": {9: ["tr2"], 11: ["s0", "s1"], 13: ["eu0", "eu1"], 16: ["fo"]},
    "DVE": {0: ["y"], 5: ["wo"], 6: ["ln2"], 8: ["xn2"], 12: ["g0", "g1"], 21: ["bt"]},
    "POOL": {1: ["gate"], 7: ["fac2"], 9: ["x1b"]},
    "SP": {21: ["store"]},
}
LOW_AFTER = next(n for n, steps in PROJ["POOL"].items() if "low" in steps)
OPENS = {"cols": ["cols"], "cols2": ["cols2"], "bias": ["bias"], "tr1": ["tr1"], "u0a": ["u0"], "u1a": ["u1"], "z0": ["z0"], "z1": ["z1"],
         "xd": ["xd"], "dt": ["dt0", "dt1"], "wo": ["wo"], "tr2": ["tr2"], "s0": ["s0"], "s1": ["s1"], "g0": ["g0"],
         "g1": ["g1"], "eu0": ["eu0"], "eu1": ["eu1"], "fo0": ["fo"], "bt": ["bt"]}


def order(engine):
    yield from FIRST[engine]
    for b in range(SEQS):
        for n in range(N):
            yield ("unit", b, n)
            if b > 1:
                yield from ((s, b - 2) for s in FFN[engine].get(n + N, []))
            if b > 0:
                yield from ((s, b - 1) for s in FFN[engine].get(n, []))
            if b < SEQS - 1:
                yield from ((s, b + 1) for s in PROJ[engine].get(n, []))
    for n in range(2 * N):
        yield from ((s, SEQS - 2) for s in FFN[engine].get(n + N, []))
        yield from ((s, SEQS - 1) for s in FFN[engine].get(n, []))


def bank_uses():
    names = [(name, item[1]) for item in order("PE") if item[0] in OPENS for name in OPENS[item[0]]]
    return {name: u for u, name in enumerate(names)}


def experts_of(j):
    return [(11 * j + 7919 * k) % EXPERTS for k in range(2)]


def classes_of(e):
    return [next(j for j in range(8) if experts_of(j)[k] == e) for k in range(2)]


def build(nc, x, ln_g, ln_b, W_in, conv_w, conv_b, W_xp, W_dt, b_dt, A_log, D_param, W_out, res_scale,
          sw1, sb1, sw3, sb3, sw2, sb2, w1, b1, w2, b2, route, out):
    f32, bf16 = mybir.dt.float32, mybir.dt.bfloat16
    ALU, ACT = mybir.AluOpType, mybir.ActivationFunctionType
    USES = bank_uses()
    b_scratch = nc.dram_tensor("b_scratch", (SEQS, N, T), f32, kind="Internal").ap()

    with ExitStack() as ctx:
        def sb(name, shape, dt=f32):
            return ctx.enter_context(nc.sbuf_tensor(name, shape, dt))

        def ps(name, shape):
            return ctx.enter_context(nc.psum_tensor(name, shape, f32))

        def sem(name):
            return ctx.enter_context(nc.semaphore(name))

        ident = sb("ident", [128, 128])
        sel = sb("sel", [SPLIT, N])
        csel = sb("csel", [SPLIT, N, 128], bf16)
        vec_rows, vec_rows2 = sb("vec_rows", [VECS1, 128]), sb("vec_rows2", [VECS - VECS1, 128])
        cols = sb("cols", [128, VECS])
        g_col, b_col = cols[:, 0:1], cols[:, 1:2]
        cb_col, dtb_col, d_col, sb1_col, sb3_col = (cols[:, 2 + 2 * i:4 + 2 * i] for i in range(5))
        b1_col = cols[:, 12:VECS]
        w_in = sb("w_in", [128, 2 * E])
        w_conv = sb("w_conv", [128, TAPS, E])
        xp_in = sb("xp_in", [128, HALF, R + 2 * N])
        w_xp = sb("w_xp", [128, HALF, ROWS])
        w_dt = sb("w_dt", [ROWS, E])
        a_log, a_exp, a_neg = sb("a_log", [128, HALF, N]), sb("a_exp", [128, HALF, N]), sb("a_neg", [128, HALF, N])
        w_out = sb("w_out", [128, HALF, D])
        rs_col = sb("rs_col", [128, 1])
        w_s1, w_s3, w_s2 = sb("w_s1", [128, HID]), sb("w_s3", [128, HID]), sb("w_s2", [128, HALF, D])
        w_e1, w_e2h = sb("w_e1", [128, EXPERTS, 128]), sb("w_e2h", [128, EXPERTS, 128])
        bias_rows, route_sb = sb("bias_rows", [EXPERTS + 1, D]), sb("route_sb", [EXPERTS + 1, CH, 128])
        bias_tok = sb("bias_tok", [128, CH, D])
        k_eps, k_mhalf, k_one, k_mone = (sb(n, [128, SEQS, CH]) for n in ("k_eps", "k_mhalf", "k_one", "k_mone"))

        xin = sb("xin", [128, SEQS, CH, D])
        stat1, stat2 = sb("stat1", [128, SEQS, CH, 6]), sb("stat2", [128, SEQS, CH, 6])
        mv1, mv2 = sb("mv1", [128, SEQS, CH, 2]), sb("mv2", [128, SEQS, CH, 2])
        tiny = sb("tiny", [128, 16, SEQS, CH])
        xnT = sb("xnT", [128, SEQS, KEEP])
        u2, gz = sb("u2", [128, 2, HALF, T]), sb("gz", [128, 2, HALF, T])
        small = sb("small", [ROWS, 2, T])
        cparts = sb("cparts", [SPLIT, 2, T], bf16)
        crest = sb("crest", [SPLIT, T])
        cmid = sb("cmid", [SPLIT, T], bf16)
        bexp, brelu, bln, bcor = (sb(n, [128, HALF, T]) for n in ("bexp", "brelu", "bln", "bcor"))
        dt, wdt = sb("dt", [128, 2, HALF, T]), sb("wdt", [128, 2, HALF, T])
        bbc = sb("bbc", [128, RING * STATES, T])
        drive = sb("drive", [128, 3, HALF, T])
        h = sb("h", [128, 2, HALF, T])
        hc = sb("hc", [128, 2, HALF, T])
        xn = hc[:, :, :, :].rearrange("p r h t -> p (r h t)").rearrange("p (b c d) -> p b c d", b=SEQS, c=CH)
        yd, yg = sb("yd", [128, HALF, T]), sb("yg", [128, HALF, T])
        taps = yd[:, :, :].rearrange("p h t -> p (h t)").rearrange("p (e k) -> p e k", k=TAPS)
        w_e2 = yg[:, :, :].rearrange("p h t -> p (h t)").rearrange("p (e c) -> p e c", e=EXPERTS)
        x1, x1b = sb("x1", [128, CH, D]), sb("x1b", [128, CH, D])
        xn2, xT = sb("xn2", [128, CH, D]), sb("xT", [128, T])
        hs1, hs = sb("hs1", [128, HALF, T]), sb("hs", [128, HALF, T])
        he = sb("he", [128, EXPERTS, 2 * CLASS])
        fo, res = sb("fo", [128, T]), sb("res", [128, 2, CH, D])

        decay = [ps(f"decay{i}", [128, T]) for i in range(3)]
        cbc = ps("cbc", [128, T])
        yacc = ps("yacc", [128, HALF, T])
        bank = [ps(f"bank{i}", [128, T]) for i in range(2)]

        x_in = [sem(f"x_in{b}") for b in range(SEQS)]
        in_vecs, in_vecs2, in_w_in, in_w_mid, in_w_scan, in_w_ffn = (
            sem(n) for n in ("in_vecs", "in_vecs2", "in_w_in", "in_w_mid", "in_w_scan", "in_w_ffn"))
        const_ok, pad_ok, conv_ok, xpz_ok, xpw_ok = (sem(n) for n in ("const_ok", "pad_ok", "conv_ok", "xpz_ok", "xpw_ok"))
        a_ok, aneg_ok, e2h_ok, bias_ok, cols_ok = (sem(n) for n in ("a_ok", "aneg_ok", "e2h_ok", "bias_ok", "cols_ok"))
        cols2_ok, sel_ok, warm_ok = sem("cols2_ok"), sem("sel_ok"), sem("warm_ok")
        stat1_ok, mv1_ok, fac1_ok, facr_ok, stat2_ok, mv2_ok, fac2_ok = (
            sem(n) for n in ("stat1_ok", "mv1_ok", "fac1_ok", "facr_ok", "stat2_ok", "mv2_ok", "fac2_ok"))
        pool_chain = sem("pool_chain")
        xn_ok, xres_ok, xnT_ok, u2_ok, gz_ok = (sem(n) for n in ("xn_ok", "xres_ok", "xnT_ok", "u2_ok", "gz_ok"))
        small_ok, hi_ok, rest_ok, mid_ok, low_ok = (sem(n) for n in ("small_ok", "hi_ok", "rest_ok", "mid_ok", "low_ok"))
        b_out = sem("b_out")
        bbc_in = [sem(f"bbc_in{i}") for i in range(RING)]
        babs_ok, brelu_ok, bexp_ok, bln_ok = (sem(n) for n in ("babs_ok", "brelu_ok", "bexp_ok", "bln_ok"))
        bcor_ok, bcor2_ok, bsum_ok, dt_ok, wdt_ok = (sem(n) for n in ("bcor_ok", "bcor2_ok", "bsum_ok", "dt_ok", "wdt_ok"))
        filled = sem("filled")
        freed = [sem(f"freed{i}") for i in range(2)]
        decay_ok, drive_ok, scan_ok, hc_ok, cbc_ok, yacc_ok = (
            sem(n) for n in ("decay_ok", "drive_ok", "scan_ok", "hc_ok", "cbc_ok", "yacc_ok"))
        yd_ok, yg_ok, x1_ok, x1b_ok, xn2_ok, xT_ok = (sem(n) for n in ("yd_ok", "yg_ok", "x1_ok", "x1b_ok", "xn2_ok", "xT_ok"))
        hs1_ok, hs_ok, he_ok, fo_ok, res_ok = (sem(n) for n in ("hs1_ok", "hs_ok", "he_ok", "fo_ok", "res_ok"))
        stored = sem("stored")

        def tokens(v):
            return v.rearrange("(i c jj) d -> jj i c d", c=CH, jj=2)

        def softplus_end(eng, on, s, b):
            if s == "sum":
                eng.wait_ge(bln_ok, b + 1)
                eng.wait_ge(brelu_ok, 2 * (b + 1))
                on.tensor_tensor(out=bln[:, :, :], in0=bln[:, :, :], in1=brelu[:, :, :], op=ALU.add).then_inc(bsum_ok, 1)
            elif s == "dt":
                eng.wait_ge(bcor2_ok, b + 1)
                eng.wait_ge(bsum_ok, b + 1)
                on.tensor_tensor(out=dt[:, b % 2], in0=bln[:, :, :], in1=bcor[:, :, :], op=ALU.add).then_inc(dt_ok, 1)
            else:
                eng.wait_ge(dt_ok, b + 1)
                if b == 0:
                    eng.wait_ge(u2_ok, 2)
                on.tensor_tensor(out=wdt[:, b % 2], in0=dt[:, b % 2], in1=u2[:, b % 2], op=ALU.mult).then_inc(wdt_ok, 1)

        def gate(eng, on, b):
            eng.wait_ge(yd_ok, 2 * (b + 1))
            if b == 0:
                eng.wait_ge(e2h_ok, 1)
            if b >= 1:
                eng.wait_ge(x1_ok, b)
            on.tensor_tensor(out=yg[:, :, :], in0=yd[:, :, :], in1=gz[:, b % 2], op=ALU.mult).then_inc(yg_ok, 1)

        block = ctx.enter_context(nc.Block())

        @block.sync
        def _(sp):
            for b in range(SEQS):
                for jj in range(2):
                    sp.dma_start(xin[64 * jj:64 * jj + 64, b], tokens(x[b])[jj]).then_inc(x_in[b], 16)
                if b == 0:
                    sp.dma_start(w_in[:, :], W_in).then_inc(in_w_in, 16)
                    sp.dma_start(taps.rearrange("p e k -> p (e k)"),
                                 conv_w.rearrange("e k -> (e k)").partition_broadcast(128)).then_inc(in_w_in, 16)
            for i, vec in enumerate((D_param, sb1, sb3, b1)):
                src = vec if len(vec.shape) == 2 else vec.rearrange("(h p) -> h p", p=128)
                sp.dma_start(vec_rows2[2 * i:2 * i + src.shape[0], :], src).then_inc(in_vecs2, 16)
            sp.dma_start(bias_rows[0:EXPERTS, :], b2).then_inc(in_w_ffn, 16)
            sp.dma_start(bias_rows[EXPERTS:EXPERTS + 1, :], sb2.rearrange("(o d) -> o d", o=1)).then_inc(in_w_ffn, 16)
            sp.dma_start(route_sb[:, :, :], route).then_inc(in_w_ffn, 16)
            sp.dma_start(w_out[:, :, :], W_out.rearrange("(h p) d -> p h d", p=128)).then_inc(in_w_ffn, 16)
            sp.dma_start(w_s1[:, :], sw1).then_inc(in_w_ffn, 16)
            sp.dma_start(w_s3[:, :], sw3).then_inc(in_w_ffn, 16)
            sp.dma_start(w_s2[:, :, :], sw2.rearrange("(h p) d -> p h d", p=128)).then_inc(in_w_ffn, 16)
            sp.dma_start(w_e1[:, :, :], w1.rearrange("e c h -> c e h")).then_inc(in_w_ffn, 16)
            sp.dma_start(w_e2, w2.rearrange("e h c -> h e c")).then_inc(in_w_ffn, 16)
            sp.dma_start(rs_col[:, :], res_scale.partition_broadcast(128)).then_inc(in_w_ffn, 16)

            def load_b(g):
                b, n = divmod(g, N)
                if g >= RING * STATES:
                    sp.wait_ge(drive_ok, g + STATES - RING * STATES)
                at = g % (RING * STATES)
                sp.dma_start(bbc[:, at:at + STATES, :].rearrange("p n t -> p (n t)"),
                             b_scratch[b, n:n + STATES, :].rearrange("n t -> (n t)").partition_broadcast(128))\
                  .then_inc(bbc_in[g // STATES % RING], 16)

            for item in order("SP"):
                if item[0] == "unit":
                    g = N * item[1] + item[2] + AHEAD
                    if g % STATES == 0 and g < N * SEQS:
                        load_b(g)
                if item[0] == "b_out":
                    b = item[1]
                    sp.wait_ge(small_ok, b + 1)
                    sp.dma_start(b_scratch[b], small[ROW_B:ROW_B + N, b % 2, :]).then_inc(b_out, 16)
                    sp.wait_ge(b_out, 16 * (b + 1))
                    if b == 0:
                        for g in range(0, AHEAD, STATES):
                            load_b(g)
                if item[0] == "store":
                    b = item[1]
                    sp.wait_ge(res_ok, b + 1)
                    for jj in range(2):
                        sp.dma_start(tokens(out[b])[jj], res[64 * jj:64 * jj + 64, b % 2]).then_inc(stored, 16)
            sp.wait_ge(stored, 32 * SEQS)

        @block.gpsimd
        def _(pool):
            chain, tt = [0], nc.gpsimd.tensor_tensor

            def link(ins):
                chain[0] += 1
                ins.then_inc(pool_chain, 1)
                pool.wait_ge(pool_chain, chain[0])

            pool.dma_start(xp_in[:, :, :], W_xp.rearrange("(h p) r -> p h r", p=128)).then_inc(in_w_mid, 16)
            pool.dma_start(w_dt[ROW_DT:ROWS, :], W_dt).then_inc(in_w_mid, 16)
            pool.dma_start(a_log[:, :, :], A_log.rearrange("(h p) n -> p h n", p=128)).then_inc(in_w_scan, 16)

            nc.gpsimd.memset(k_eps[:, :, :], EPS)
            nc.gpsimd.memset(k_mhalf[:, :, :], -0.5)
            nc.gpsimd.memset(k_one[:, :, :], 1.0)
            nc.gpsimd.memset(k_mone[:, :, :], -1.0)
            link(nc.gpsimd.memset(ident[:, :], 0.0))
            nc.gpsimd.affine_select(out=ident[:, :], in_=ident[:, :], compare_op=ALU.not_equal, fill=1.0, base=0,
                                    pattern=[[-1, 128]], channel_multiplier=1).then_inc(const_ok, 1)
            nc.gpsimd.memset(xnT[:, :, 0:TAPS - 1], 0.0).then_inc(pad_ok, 1)

            def factors(mv, seqs, k):
                f = [tiny[:, k + i, seqs, :] for i in range(8)]
                link(tt(out=f[0], in0=mv[:, seqs, :, 1], in1=k_eps[:, seqs, :], op=ALU.add))
                link(tt(out=f[1], in0=f[0], in1=k_mhalf[:, seqs, :], op=ALU.pow))
                link(tt(out=f[2], in0=mv[:, seqs, :, 0], in1=k_mone[:, seqs, :], op=ALU.mult))
                return f

            def unit(g):
                b, n = divmod(g, N)
                if n == 0:
                    pool.wait_ge(wdt_ok, b + 1)
                if g % STATES == 0:
                    pool.wait_ge(bbc_in[g // STATES % RING], 16 * (g // STATES // RING + 1))
                if g >= 3:
                    pool.wait_ge(scan_ok, 2 * (g - 2))
                nc.gpsimd.tensor_tensor(out=drive[:, g % 3], in0=wdt[:, b % 2],
                                        in1=bbc[:, g % (RING * STATES), :].unsqueeze(1).broadcast_to([128, HALF, T]),
                                        op=ALU.mult).then_inc(drive_ok, 1)

            for item in order("POOL"):
                s, b = item[0], item[1]
                if s == "unit":
                    g = N * b + item[2]
                    if g == 0:
                        unit(0)
                    if g + 1 < N * SEQS:
                        unit(g + 1)
                elif s == "csel":
                    link(nc.gpsimd.memset(sel[:, :], 0.0))
                    for q in ROW_C:
                        ins = nc.gpsimd.affine_select(out=sel[:, :], in_=sel[:, :], compare_op=ALU.not_equal,
                                                      fill=1.0, base=-q, pattern=[[-1, N]], channel_multiplier=1)
                        if q == ROW_C[-1]:
                            ins.then_inc(sel_ok, 1)
                        else:
                            link(ins)
                elif s == "fac1":
                    seqs = slice(0, 1) if b == 0 else slice(1, SEQS)
                    pool.wait_ge(mv1_ok, CH if b == 0 else CH * SEQS)
                    f = factors(mv1, seqs, 0)
                    link(tt(out=f[3], in0=f[1], in1=f[1], op=ALU.mult))
                    link(tt(out=f[4], in0=f[3], in1=mv1[:, seqs, :, 1], op=ALU.mult))
                    link(tt(out=f[5], in0=f[4], in1=k_eps[:, seqs, :], op=ALU.add))
                    link(tt(out=f[6], in0=f[5], in1=k_mhalf[:, seqs, :], op=ALU.pow))
                    link(tt(out=f[7], in0=f[6], in1=f[1], op=ALU.mult))
                    tt(out=tiny[:, 12, seqs, :], in0=f[7], in1=f[2], op=ALU.mult).then_inc(fac1_ok, 1)
                    tt(out=tiny[:, 13, seqs, :], in0=f[1], in1=k_one[:, seqs, :], op=ALU.add)
                    tt(out=tiny[:, 14, seqs, :], in0=f[1], in1=f[2], op=ALU.mult).then_inc(facr_ok, 1)
                elif s == "rest":
                    pool.wait_ge(hi_ok, b + 1)
                    tt(out=crest[:, :], in0=small[0:SPLIT, b % 2], in1=cparts[:, b % 2],
                       op=ALU.subtract).then_inc(rest_ok, 1)
                elif s == "low":
                    pool.wait_ge(rest_ok, b + 1)
                    if b > 0:
                        pool.wait_ge(drive_ok, N * (b - 1) + LOW_AFTER + 2)
                    pool.wait_ge(mid_ok, 2 * (b + 1))
                    tt(out=cparts[64:96, b % 2], in0=crest[64:96, :], in1=cmid[64:96, :],
                       op=ALU.subtract).then_inc(low_ok, 1)
                    pool.wait_ge(low_ok, b + 1)
                elif s in ("sum", "dt", "wdt"):
                    softplus_end(pool, nc.gpsimd, s, b)
                elif s == "gate" and b < SEQS - 1:
                    gate(pool, nc.gpsimd, b)
                elif s == "fac2":
                    pool.wait_ge(mv2_ok, CH * (b + 1))
                    f = factors(mv2, slice(b, b + 1), 8)
                    tt(out=f[3], in0=f[1], in1=f[2], op=ALU.mult).then_inc(fac2_ok, 1)
                elif s == "x1b":
                    if b == 0:
                        pool.wait_ge(bias_ok, 1)
                    if b >= 1:
                        pool.wait_ge(res_ok, b)
                    tt(out=x1b[:, :, :], in0=x1[:, :, :], in1=bias_tok[:, :, :], op=ALU.add).then_inc(x1b_ok, 1)

        @block.scalar
        def _(act):
            fn = nc.scalar.activation
            for i, vec in enumerate((ln_g, ln_b, conv_b, b_dt)):
                row = i if i < 2 else 2 * i - 2
                src = vec.rearrange("(h p) -> h p", p=128)
                act.dma_start(vec_rows[row:row + src.shape[0], :], src).then_inc(in_vecs, 16)

            def full(step, b):
                u = USES[step, b]
                act.wait_ge(filled, u + 1)
                return bank[u % 2], u % 2

            def log_exp():
                nc.scalar.preload_act_table_set("natural_log_exp_and_others")

            def decays(g):
                b, n = divmod(g, N)
                if n == 0:
                    act.wait_ge(dt_ok, b + 1)
                for hf in range(HALF):
                    r = 2 * g + hf
                    if r >= 3:
                        act.wait_ge(scan_ok, r - 2)
                    fn(decay[r % 3][:, :], dt[:, b % 2, hf, :], ACT.Exp,
                       scale=a_neg[:, hf, n:n + 1]).then_inc(decay_ok, 1)

            for item in order("ACT"):
                s, b = item[0], item[1]
                if s == "unit":
                    g = N * b + item[2]
                    if g == 0:
                        log_exp()
                        act.wait_ge(aneg_ok, 1)
                        act.wait_ge(warm_ok, 1)
                        decays(0)
                    if g + 1 < N * SEQS:
                        decays(g + 1)
                elif s == "cols":
                    act.wait_ge(in_w_scan, 16)
                    fn(a_exp[:, :, :], a_log[:, :, :], ACT.Exp).then_inc(a_ok, 1)
                elif s == "xn":
                    for q in ([0] if b == 0 else range(1, SEQS)):
                        act.wait_ge(fac1_ok, min(q, 1) + 1)
                        for c in range(CH):
                            ins = fn(xn[:, q, c, :], xin[:, q, c, :], ACT.Identity,
                                     scale=tiny[:, 7, q, c:c + 1], bias=tiny[:, 12, q, c:c + 1])
                        ins.then_inc(xn_ok, 1)
                elif s == "tr1":
                    m, k = full("tr1", b)
                    if b == 0:
                        act.wait_ge(cols_ok, 1)
                    fn(xnT[:, b, TAPS - 1:].rearrange("p (i j) -> p j i", j=8),
                       m[:, :].rearrange("p (j i) -> p j i", j=8), ACT.Identity,
                       scale=g_col, bias=b_col).then_inc(xnT_ok, 1)
                    act.wait_ge(xnT_ok, b + 1)
                    act.sem_inc(freed[k], 1)
                elif s in ("u0", "u1"):
                    m, k = full(s, b)
                    hf = int(s[1])
                    if b >= 2:
                        act.wait_ge(yd_ok, 2 * (b - 1))
                    fn(u2[:, b % 2, hf], m[:, :], ACT.Silu, bias=cb_col[:, hf:hf + 1]).then_inc(u2_ok, 1)
                    if b > 0 and hf == 1:
                        log_exp()
                    act.wait_ge(u2_ok, 2 * b + hf + 1)
                    act.sem_inc(freed[k], 1)
                elif s in ("z0", "z1"):
                    m, k = full(s, b)
                    hf = int(s[1])
                    if b >= 2:
                        act.wait_ge(yg_ok, b - 1)
                    fn(gz[:, b % 2, hf].rearrange("p (j i) -> p j i", j=8),
                       m[:, :].rearrange("p (i j) -> p j i", j=8), ACT.Silu).then_inc(freed[k], 1)
                    if b > 0 and hf == 1:
                        log_exp()
                elif s == "xd":
                    m, k = full(s, b)
                    fn(small[:, b % 2], m[0:ROWS, :], ACT.Identity).then_inc(small_ok, 1)
                    act.wait_ge(small_ok, b + 1)
                    act.sem_inc(freed[k], 1)
                    fn(cparts[:, b % 2], small[0:SPLIT, b % 2], ACT.Identity).then_inc(hi_ok, 1)
                elif s == "mid":
                    act.wait_ge(rest_ok, b + 1)
                    fn(cparts[32:64, b % 2], crest[32:64, :], ACT.Identity).then_inc(mid_ok, 1)
                    fn(cmid[64:96, :], crest[64:96, :], ACT.Identity).then_inc(mid_ok, 1)
                elif s == "relu":
                    if b == 0:
                        log_exp()
                    for hf in range(HALF):
                        m, k = full(f"dt{hf}", b)
                        if b >= 1:
                            act.wait_ge(bcor2_ok, b)
                            act.wait_ge(dt_ok, b)
                        fn(bexp[:, hf], m[:, :], ACT.Abs, bias=dtb_col[:, hf:hf + 1]).then_inc(babs_ok, 1)
                        fn(brelu[:, hf], m[:, :], ACT.Relu, bias=dtb_col[:, hf:hf + 1]).then_inc(brelu_ok, 1)
                        act.wait_ge(brelu_ok, 2 * b + hf + 1)
                        act.sem_inc(freed[k], 1)
                elif s == "exp":
                    act.wait_ge(babs_ok, 2 * (b + 1))
                    fn(bexp[:, :, :], bexp[:, :, :], ACT.Exp, scale=-1.0).then_inc(bexp_ok, 1)
                elif s == "ln":
                    act.wait_ge(bexp_ok, b + 1)
                    fn(bln[:, :, :], bexp[:, :, :], ACT.Ln, bias=1.0).then_inc(bln_ok, 1)
                elif s == "tr2":
                    m, k = full(s, b)
                    fn(xT[:, :], m[:, :], ACT.Identity).then_inc(xT_ok, 1)
                    act.wait_ge(xT_ok, b + 1)
                    act.sem_inc(freed[k], 1)
                elif s in ("s0", "s1"):
                    m, k = full(s, b)
                    hf = int(s[1])
                    fn(hs1[:, hf], m[:, :], ACT.Silu, bias=sb1_col[:, hf:hf + 1]).then_inc(hs1_ok, 1)
                    if hf == 1 and b < SEQS - 1:
                        log_exp()
                    act.wait_ge(hs1_ok, 2 * b + hf + 1)
                    act.sem_inc(freed[k], 1)
                elif s in ("eu0", "eu1"):
                    m, k = full(s, b)
                    for i in range(4):
                        e = 4 * int(s[2]) + i
                        ins = fn(he[:, e, :], m[:, i * 128:(i + 1) * 128], ACT.Gelu, bias=b1_col[:, e:e + 1])
                    ins.then_inc(he_ok, 1)
                    if s == "eu1" and b < SEQS - 1:
                        log_exp()
                    act.wait_ge(he_ok, 2 * b + int(s[2]) + 1)
                    act.sem_inc(freed[k], 1)
                elif s == "fo":
                    m, k = full(s, b)
                    fn(fo[:, :], m[:, :], ACT.Identity).then_inc(fo_ok, 1)
                    act.wait_ge(fo_ok, b + 1)
                    act.sem_inc(freed[k], 1)

        @block.tensor
        def _(pe):
            mm = nc.tensor.matmul

            def take(step, b):
                u = USES[step, b]
                if u >= 2:
                    pe.wait_ge(freed[u % 2], u // 2)
                return bank[u % 2]

            def accumulate(g):
                b, n = divmod(g, N)
                pe.wait_ge(hc_ok, g + 1)
                if n == 0 and b >= 1:
                    pe.wait_ge(yd_ok, 2 * b)
                for hf in range(HALF):
                    ins = mm(yacc[:, hf, :], ident[:, :], hc[:, g % 2, hf], start=(n == 0), stop=(n == N - 1))
                ins.then_inc(yacc_ok, 1)

            for item in order("PE"):
                s, b = item[0], item[1]
                if s == "unit":
                    n = item[2]
                    g = N * b + n
                    if n == 0:
                        if b == 0:
                            pe.wait_ge(const_ok, 2)
                        pe.wait_ge(low_ok, b + 1)
                        pe.wait_ge(mid_ok, 2 * (b + 1))
                    if g >= 1:
                        pe.wait_ge(hc_ok, g)
                    mm(cbc[:, :], csel[:, n, :], cparts[:, b % 2], start=True, stop=True).then_inc(cbc_ok, 1)
                    if n >= 1:
                        accumulate(g - 1)
                elif s == "warm":
                    pe.wait_ge(const_ok, 1)
                    for i in range(WARM):
                        ins = mm(decay[0][:, 0:128], ident[:, :], ident[:, :], start=True, stop=True)
                    ins.then_inc(warm_ok, 1)
                elif s == "cols":
                    pe.wait_ge(in_vecs, 16 * 4)
                    nc.tensor.transpose(take(s, b)[:, 0:VECS1], vec_rows[:, :], ident[0:VECS1, 0:VECS1]).then_inc(filled, 1)
                elif s == "cols2":
                    pe.wait_ge(in_vecs2, 16 * 4)
                    rows = VECS - VECS1
                    nc.tensor.transpose(take(s, b)[:, 0:rows], vec_rows2[:, :], ident[0:rows, 0:rows]).then_inc(filled, 1)
                elif s == "bias":
                    pe.wait_ge(in_w_ffn, 16 * 10)
                    m = take(s, b)
                    for c in range(CH):
                        ins = mm(m[:, c * D:(c + 1) * D], route_sb[:, c, :], bias_rows[:, :], start=True, stop=True)
                    ins.then_inc(filled, 1)
                elif s == "tr1":
                    m = take(s, b)
                    if b == 0:
                        pe.wait_ge(const_ok, 1)
                    pe.wait_ge(xn_ok, b + 1)
                    for c in range(CH):
                        ins = nc.tensor.transpose(m[:, c * 128:(c + 1) * 128], xn[:, b, c, :], ident[:, :])
                    ins.then_inc(filled, 1)
                elif s in ("u0a", "u0b", "u1a", "u1b"):
                    hf = int(s[1])
                    m = take(s[:2], b) if s[2] == "a" else bank[USES[s[:2], b] % 2]
                    if s == "u0a":
                        if b == 0:
                            pe.wait_ge(conv_ok, 1)
                            pe.wait_ge(pad_ok, 1)
                        pe.wait_ge(xnT_ok, b + 1)
                    for k in ((0, 1) if s[2] == "a" else (2, 3)):
                        ins = mm(m[:, :], w_conv[:, k, hf * 128:(hf + 1) * 128], xnT[:, b, k:k + T],
                                 start=(k == 0), stop=(k == TAPS - 1))
                    if s[2] == "b":
                        ins.then_inc(filled, 1)
                elif s in ("z0", "z1"):
                    m = take(s, b)
                    hf = int(s[1])
                    mm(m[:, :], w_in[:, E + hf * 128:E + (hf + 1) * 128], xnT[:, b, TAPS - 1:],
                       start=True, stop=True).then_inc(filled, 1)
                elif s == "xd":
                    m = take(s, b)
                    if b == 0:
                        pe.wait_ge(xpw_ok, 9 + 1)
                    pe.wait_ge(u2_ok, 2 * (b + 1))
                    for hf in range(HALF):
                        ins = mm(m[0:ROWS, :], w_xp[:, hf, :], u2[:, b % 2, hf], start=(hf == 0), stop=(hf == 1))
                    ins.then_inc(filled, 1)
                elif s == "dt":
                    pe.wait_ge(small_ok, b + 1)
                    for hf in range(HALF):
                        m = take(f"dt{hf}", b)
                        mm(m[:, :], w_dt[ROW_DT:ROWS, hf * 128:(hf + 1) * 128], small[ROW_DT:ROWS, b % 2],
                           start=True, stop=True).then_inc(filled, 1)
                elif s == "y":
                    accumulate(N * b + N - 1)
                elif s == "wo":
                    m = take(s, b)
                    pe.wait_ge(yg_ok, b + 1)
                    for c in range(CH):
                        for hf in range(HALF):
                            ins = mm(m[:, c * D:(c + 1) * D], yg[:, hf, c * 128:(c + 1) * 128], w_out[:, hf, :],
                                     start=(hf == 0), stop=(hf == 1))
                    ins.then_inc(filled, 1)
                elif s == "tr2":
                    m = take(s, b)
                    pe.wait_ge(xn2_ok, CH * (b + 1))
                    for c in range(CH):
                        ins = nc.tensor.transpose(m[:, c * 128:(c + 1) * 128], xn2[:, c, :], ident[:, :])
                    ins.then_inc(filled, 1)
                elif s in ("s0", "s1", "g0", "g1"):
                    m = take(s, b)
                    hf = int(s[1])
                    pe.wait_ge(xT_ok, b + 1)
                    w = w_s1 if s[0] == "s" else w_s3
                    mm(m[:, :], w[:, hf * 128:(hf + 1) * 128], xT[:, :], start=True, stop=True).then_inc(filled, 1)
                elif s in ("eu0", "eu1"):
                    m = take(s, b)
                    for i in range(4):
                        e = 4 * int(s[2]) + i
                        for k, j in enumerate(classes_of(e)):
                            ins = mm(m[:, i * 128 + k * CLASS:i * 128 + (k + 1) * CLASS], w_e1[:, e, :],
                                     xT[:, j * CLASS:(j + 1) * CLASS], start=True, stop=True)
                    ins.then_inc(filled, 1)
                elif s == "fo0":
                    m = take("fo", b)
                    pe.wait_ge(hs_ok, 2 * (b + 1))
                    mm(m[:, :], w_s2[:, 0, :], hs[:, 0], start=True, stop=False)
                elif s == "fo1":
                    m = bank[USES["fo", b] % 2]
                    pe.wait_ge(he_ok, 2 * (b + 1))
                    if b == 0:
                        pe.wait_ge(e2h_ok, 1)
                    for e in range(EXPERTS):
                        for k, j in enumerate(classes_of(e)):
                            mm(m[:, j * CLASS:(j + 1) * CLASS], w_e2h[:, e, :],
                               he[:, e, k * CLASS:(k + 1) * CLASS], start=False, stop=False)
                elif s == "fo2":
                    m = bank[USES["fo", b] % 2]
                    mm(m[:, :], w_s2[:, 1, :], hs[:, 1], start=False, stop=True).then_inc(filled, 1)
                elif s == "bt":
                    m = take(s, b)
                    pe.wait_ge(fo_ok, b + 1)
                    for c in range(CH):
                        ins = nc.tensor.transpose(m[:, c * 128:(c + 1) * 128], fo[:, c * 128:(c + 1) * 128], ident[:, :])
                    ins.then_inc(filled, 1)

        @block.vector
        def _(dve):
            v = nc.vector

            def full(step, b):
                u = USES[step, b]
                dve.wait_ge(filled, u + 1)
                return bank[u % 2], u % 2

            def stats(src, stat, mv, stat_ok, mv_ok, b):
                for c in range(CH):
                    v.bn_stats(out=stat[:, b, c, :], in_=src[:, c, :]).then_inc(stat_ok, 1)
                for c in range(CH):
                    dve.wait_ge(stat_ok, CH * b + c + 1)
                    v.bn_aggr(out=mv[:, b, c, :], in_=stat[:, b, c, :]).then_inc(mv_ok, 1)

            v.memset(w_xp[:, :, :], 0.0).then_inc(xpz_ok, 1)

            for item in order("DVE"):
                s, b = item[0], item[1]
                if s == "unit":
                    n = item[2]
                    g = N * b + n
                    dve.wait_ge(drive_ok, g + 1)
                    for hf in range(HALF):
                        r = 2 * g + hf
                        dve.wait_ge(decay_ok, r + 1)
                        v.tensor_tensor_scan(h[:, g % 2, hf, :], decay[r % 3][:, :], drive[:, g % 3, hf], 0.0,
                                             ALU.mult, ALU.add).then_inc(scan_ok, 1)
                    dve.wait_ge(scan_ok, 2 * g + 2)
                    dve.wait_ge(cbc_ok, g + 1)
                    if g == 0:
                        dve.wait_ge(xnT_ok, SEQS)
                    if g >= 2:
                        dve.wait_ge(yacc_ok, g - 1)
                    v.tensor_tensor(out=hc[:, g % 2], in0=h[:, g % 2],
                                    in1=cbc[:, :].unsqueeze(1).broadcast_to([128, HALF, T]),
                                    op=ALU.mult).then_inc(hc_ok, 1)
                elif s == "ln1":
                    dve.wait_ge(x_in[b], 32)
                    stats(xin[:, b], stat1, mv1, stat1_ok, mv1_ok, b)
                elif s == "weights":
                    dve.wait_ge(in_w_in, 32)
                    for k in range(TAPS):
                        ins = v.tensor_tensor(out=w_conv[:, k, :], in0=w_in[:, 0:E], in1=taps[:, :, k], op=ALU.mult)
                    ins.then_inc(conv_ok, 1)
                    dve.wait_ge(in_w_mid, 32)
                    dve.wait_ge(xpz_ok, 1)
                    for hf in range(HALF):
                        for q in ROW_C:
                            v.tensor_copy(w_xp[:, hf, q:q + N], xp_in[:, hf, R + N:R + 2 * N]).then_inc(xpw_ok, 1)
                        v.tensor_copy(w_xp[:, hf, ROW_B:ROW_B + N], xp_in[:, hf, R:R + N]).then_inc(xpw_ok, 1)
                        v.tensor_copy(w_xp[:, hf, ROW_DT:ROWS], xp_in[:, hf, 0:R]).then_inc(xpw_ok, 1)
                    dve.wait_ge(a_ok, 1)
                    v.tensor_scalar(a_neg[:, :, :], a_exp[:, :, :], -1.0, None, ALU.mult).then_inc(aneg_ok, 1)
                elif s == "cols":
                    m, k = full(s, b)
                    v.tensor_copy(cols[:, 0:VECS1], m[:, 0:VECS1]).then_inc(cols_ok, 1)
                    dve.wait_ge(cols_ok, 1)
                    dve.sem_inc(freed[k], 1)
                elif s == "cols2":
                    m, k = full(s, b)
                    v.tensor_copy(cols[:, VECS1:VECS], m[:, 0:VECS - VECS1]).then_inc(cols2_ok, 1)
                    dve.wait_ge(cols2_ok, 1)
                    dve.sem_inc(freed[k], 1)
                elif s == "csel":
                    dve.wait_ge(sel_ok, 1)
                    v.tensor_copy(csel[:, :, :], sel[:, :].unsqueeze(2).broadcast_to([SPLIT, N, 128])).then_inc(const_ok, 1)
                elif s == "xres":
                    dve.wait_ge(facr_ok, min(b, 1) + 1)
                    dve.wait_ge(xn_ok, b + 1)
                    for c in range(CH):
                        v.tensor_scalar(xin[:, b, c, :], xin[:, b, c, :], tiny[:, 13, b, c:c + 1],
                                        tiny[:, 14, b, c:c + 1], ALU.mult, ALU.add).then_inc(xres_ok, 1)
                elif s == "xn2":
                    dve.wait_ge(fac2_ok, b + 1)
                    if b >= 1:
                        dve.wait_ge(xT_ok, b)
                    for c in range(CH):
                        v.tensor_scalar(xn2[:, c, :], x1[:, c, :], tiny[:, 9, b, c:c + 1],
                                        tiny[:, 11, b, c:c + 1], ALU.mult, ALU.add).then_inc(xn2_ok, 1)
                elif s == "bias":
                    m, k = full(s, b)
                    v.tensor_copy(bias_tok[:, :, :].rearrange("p c d -> p (c d)"), m[:, :]).then_inc(bias_ok, 1)
                    dve.wait_ge(bias_ok, 1)
                    dve.sem_inc(freed[k], 1)
                    v.tensor_scalar(w_e2h[:, :, :], w_e2, 0.5, None, ALU.mult).then_inc(e2h_ok, 1)
                elif s in ("sum", "dt", "wdt"):
                    softplus_end(dve, v, s, b)
                elif s == "cor":
                    dve.wait_ge(bexp_ok, b + 1)
                    if b >= 1:
                        dve.wait_ge(dt_ok, b)
                    v.tensor_scalar(bcor[:, :, :], bexp[:, :, :], 1.0, 1.0, ALU.add, ALU.subtract).then_inc(bcor_ok, 1)
                    dve.wait_ge(bcor_ok, b + 1)
                    v.tensor_tensor(out=bcor[:, :, :], in0=bexp[:, :, :], in1=bcor[:, :, :],
                                    op=ALU.subtract).then_inc(bcor2_ok, 1)
                elif s == "y":
                    dve.wait_ge(yacc_ok, N * (b + 1))
                    if b >= 1:
                        dve.wait_ge(yg_ok, b)
                    for hf in range(HALF):
                        v.scalar_tensor_tensor(out=yd[:, hf].rearrange("p (j i) -> p j i", j=8),
                                               in0=u2[:, b % 2, hf].rearrange("p (i j) -> p j i", j=8),
                                               scalar=d_col[:, hf:hf + 1],
                                               in1=yacc[:, hf, :].rearrange("p (i j) -> p j i", j=8),
                                               op0=ALU.mult, op1=ALU.add).then_inc(yd_ok, 1)
                    if b == SEQS - 1:
                        gate(dve, v, b)
                elif s == "wo":
                    m, k = full(s, b)
                    dve.wait_ge(xres_ok, CH * (b + 1))
                    if b >= 1:
                        dve.wait_ge(xn2_ok, CH * b)
                        dve.wait_ge(x1b_ok, b)
                    v.scalar_tensor_tensor(out=x1[:, :, :].rearrange("p c d -> p (c d)"), in0=m[:, :], scalar=rs_col[:, :],
                                           in1=xin[:, b].rearrange("p c d -> p (c d)"),
                                           op0=ALU.mult, op1=ALU.add).then_inc(x1_ok, 1)
                    dve.wait_ge(x1_ok, b + 1)
                    dve.sem_inc(freed[k], 1)
                elif s == "ln2":
                    stats(x1, stat2, mv2, stat2_ok, mv2_ok, b)
                elif s in ("g0", "g1"):
                    m, k = full(s, b)
                    hf = int(s[1])
                    dve.wait_ge(hs1_ok, 2 * b + hf + 1)
                    v.scalar_tensor_tensor(out=hs[:, hf], in0=m[:, :], scalar=sb3_col[:, hf:hf + 1], in1=hs1[:, hf],
                                           op0=ALU.add, op1=ALU.mult).then_inc(hs_ok, 1)
                    dve.wait_ge(hs_ok, 2 * b + hf + 1)
                    dve.sem_inc(freed[k], 1)
                elif s == "bt":
                    m, k = full(s, b)
                    dve.wait_ge(x1b_ok, b + 1)
                    if b >= 2:
                        dve.wait_ge(stored, 32 * (b - 1))
                    v.scalar_tensor_tensor(out=res[:, b % 2].rearrange("p c d -> p (c d)"), in0=m[:, :], scalar=0.5,
                                           in1=x1b[:, :, :].rearrange("p c d -> p (c d)"),
                                           op0=ALU.mult, op1=ALU.add).then_inc(res_ok, 1)
                    dve.wait_ge(res_ok, b + 1)
                    dve.sem_inc(freed[k], 1)


_INS = ['L0_attn_x', 'L0_attn_ln_g', 'L0_attn_ln_b', 'L0_attn_W_in', 'L0_attn_conv_w', 'L0_attn_conv_b',
        'L0_attn_W_xp', 'L0_attn_W_dt', 'L0_attn_b_dt', 'L0_attn_A_log', 'L0_attn_D_param', 'L0_attn_W_out',
        'L0_attn_res_scale', 'L0_ffn_sw1', 'L0_ffn_sb1', 'L0_ffn_sw3', 'L0_ffn_sb3', 'L0_ffn_sw2', 'L0_ffn_sb2',
        'L0_ffn_w1', 'L0_ffn_b1', 'L0_ffn_w2', 'L0_ffn_b2']


def kernel(**inputs):
    import numpy as _np
    import concourse.bacc as _bacc
    from concourse import mybir as _mybir
    from concourse.bass_utils import run_bass_kernel_spmd as _run

    nc = _bacc.Bacc("TRN2", target_bir_lowering=False, num_devices=1)
    arrays, args = {}, []
    for name in _INS:
        a = _np.ascontiguousarray(inputs[name])
        arrays[f"in_{name}_dram"] = a
        args.append(nc.dram_tensor(f"in_{name}_dram", a.shape, _mybir.dt.from_np(a.dtype), kind="ExternalInput").ap())
    route = _np.zeros((EXPERTS + 1, CH, 128), _np.float32)
    for j in range(8):
        at = slice(64 * (j % 2), 64 * (j % 2) + 64)
        for e in experts_of(j):
            route[e, j // 2, at] = 0.25
        route[EXPERTS, j // 2, at] = 0.5
    arrays["route_dram"] = route
    args.append(nc.dram_tensor("route_dram", route.shape, _mybir.dt.float32, kind="ExternalInput").ap())
    args.append(nc.dram_tensor("out_0_dram", (SEQS, T, D), _mybir.dt.float32, kind="ExternalOutput").ap())
    build(nc, *args)
    r = _run(nc, [arrays], core_ids=[0])
    return r.results[0]["out_0_dram"]
```

```python
import concourse.bass as bass
from concourse import mybir
from contextlib import ExitStack

SEQS, T, D = 4, 512, 128
E, N, R, TAPS = 256, 16, 8, 4
HALF = 2
CH = T // 128
EXPERTS, CLASS = 8, T // 8
HID = 256
VECS = 2 + 5 * HALF + EXPERTS
VECS1 = 2 + 2 * HALF
EPS = 1e-5
KEEP = T + TAPS - 1
STATES = 2
RING = 4
WARM = 10
DECAYS, DRIVES, HCS, BANKS = 8, 4, 3, 4
LEAD = 2
AHEAD = 6

ROW_DT, ROWS = 2 * N, 2 * N + R

FIRST = {
    "PE": [("warm", 0), ("cols", 0), ("tr1", 0), ("u0a", 0), ("u0b", 0), ("u1a", 0), ("u1b", 0), ("z0", 0), ("z1", 0),
           ("xd", 0), ("tr1", 1), ("dt", 0), ("tr1", 2), ("tr1", 3)],
    "ACT": [("cols", 0), ("tr1", 0), ("a_exp", 0), ("u0", 0), ("u1", 0), ("z0", 0), ("z1", 0), ("xd", 0), ("soft", 0)],
    "DVE": [("ln1", 0), ("xn", 0), ("w_conv", 0), ("w_xp", 0), ("ln1", 1), ("ln1", 2), ("ln1", 3), ("a_neg", 0),
            ("xn", 1), ("xn", 2), ("xn", 3), ("tr1", 1), ("soft", 0)],
    "POOL": [("fac1", 0), ("fac1", 1), ("facr", 0)],
    "SP": [("bc_out", 0)],
}
EARLY = {
    "PE": {8: [("cols2", 0)], 9: [("bias", 0)]},
    "DVE": {10: [("cols2", 0)], 11: [("bias", 0)]},
    "ACT": {0: [("tr1", 2), ("tr1", 3)], 1: [("xres", 0)], 2: [("xres", 1)], 12: [("xres", 2)], 13: [("xres", 3)]},
    "POOL": {}, "SP": {},
}
PROJ = {
    "PE": {-3: ["u0a"], -2: ["u0b"], -1: ["u1a"], 1: ["u1b", "z1"], 2: ["z0"], 3: ["xd"], 4: ["dt"]},
    "ACT": {3: ["uz"], 5: ["xd"], 6: ["relu"], 8: ["exp", "ln"], 9: ["one"]},
    "DVE": {},
    "POOL": {12: ["cor", "sum", "dt"], 13: ["wdt"]},
    "SP": {8: ["bc_out"]},
}
FFN = {
    "PE": {0: ["y"], 2: ["wo"], 8: ["tr2"], 10: ["s0", "g0", "g1"], 11: ["s1"], 12: ["eu0", "eu1", "fo0"],
          13: ["fo1"], 14: ["fo2"], 18: ["bt"]},
    "ACT": {10: ["tr2"], 11: ["s"], 12: ["eu"], 17: ["fo"]},
    "DVE": {1: ["y"], 4: ["wo"], 6: ["ln2"], 8: ["xn2"], 11: ["g0", "g1"], 21: ["bt"]},
    "POOL": {2: ["gate"], 7: ["fac2"], 9: ["x1b"]},
    "SP": {20: ["store"]},
}
FFN_LATE = {
    "PE": {0: ["y"], 2: ["wo"], 8: ["tr2", "s0", "eu0"], 10: ["s1", "g0", "eu1"], 13: ["g1"]},
    "ACT": {10: ["tr2"], 12: ["s", "eu"]},
    "DVE": {1: ["y"], 3: ["wo"], 4: ["ln2"], 7: ["xn2"], 11: ["g0"], 14: ["g1"]},
    "POOL": {1: ["gate"], 7: ["fac2", "x1b"]},
    "SP": {},
}
LAST = {
    "PE": [("y", 3), ("fo0", 2), ("wo", 3), ("fo1", 2), ("fo2", 2), ("bt", 2), ("tr2", 3), ("s0", 3), ("s1", 3),
           ("eu0", 3), ("eu1", 3), ("g0", 3), ("g1", 3), ("fo0", 3), ("fo1", 3), ("fo2", 3), ("bt", 3)],
    "ACT": [("silu", 3), ("fo", 2), ("tr2", 3), ("s", 3), ("gelu", 3), ("eu", 3), ("fo", 3), ("store", 3)],
    "DVE": [("y", 3), ("wo", 3), ("ln2", 3), ("xn2", 3), ("bt", 2), ("g0", 3), ("g1", 3), ("bt", 3)],
    "POOL": [("fac2", 3), ("x1b", 3)],
    "SP": [("store", 2), ("store", 3)],
}
TAKES = {"u0a": ["u0"], "u1a": ["u1"], "dt": ["dt0", "dt1"], "fo0": ["fo"],
         **{s: [s] for s in ("cols", "cols2", "bias", "tr1", "z0", "z1", "xd", "wo", "tr2", "s0", "s1", "g0", "g1", "eu0",
                             "eu1", "bt")}}
FILLS = {"u0b": ["u0"], "u1b": ["u1"], "fo2": ["fo"], **{s: v for s, v in TAKES.items() if s not in ("u0a", "u1a", "fo0")}}


def order(engine):
    last = SEQS - 1
    yield from FIRST[engine]
    yield from ((s, 1) for n in range(-N, 0) for s in PROJ[engine].get(n, []))
    for b in range(SEQS):
        for n in range(N):
            yield ("unit", b, n)
            if b == 0:
                yield from EARLY[engine].get(n, [])
            if b < last:
                yield from ((s, b + 1) for s in PROJ[engine].get(n, []))
            if b + 2 <= last:
                yield from ((s, b + 2) for s in PROJ[engine].get(n - N, []))
            if b > 1:
                yield from ((s, b - 2) for s in FFN[engine].get(n + N, []))
            if b > 0:
                yield from ((s, b - 1) for s in (FFN if b < last else FFN_LATE)[engine].get(n, []))
    yield from LAST[engine]


def numbers(steps):
    names = [(name, item[1]) for item in order("PE")
             if item[0] in steps and (item[0] != "tr1" or item[1] == 0) for name in steps[item[0]]]
    return {name: u for u, name in enumerate(names)}


def experts_of(j):
    return [(11 * j + 7919 * k) % EXPERTS for k in range(2)]


def classes_of(e):
    first, second = [j for j in range(8) if e in experts_of(j)]
    return slice(first, second + 1, second - first)


def build(nc, x, ln_g, ln_b, W_in, conv_w, conv_b, W_xp, W_dt, b_dt, A_log, D_param, W_out, res_scale,
          sw1, sb1, sw3, sb3, sw2, sb2, w1, b1, w2, b2, route, out):
    f32 = mybir.dt.float32
    ALU, ACT = mybir.AluOpType, mybir.ActivationFunctionType
    USES, FILLED = numbers(TAKES), numbers(FILLS)
    bc_scratch = nc.dram_tensor("bc_scratch", (SEQS, N, 2, T), f32, kind="Internal").ap()

    with ExitStack() as ctx:
        def sb(name, shape, dt=f32):
            return ctx.enter_context(nc.sbuf_tensor(name, shape, dt))

        def ps(name, shape):
            return ctx.enter_context(nc.psum_tensor(name, shape, f32))

        def sem(name):
            return ctx.enter_context(nc.semaphore(name))

        ident = sb("ident", [128, 128])
        vec_rows, vec_rows2 = sb("vec_rows", [VECS1, 128]), sb("vec_rows2", [VECS - VECS1, 128])
        cols = sb("cols", [128, VECS])
        g_col, b_col = cols[:, 0:1], cols[:, 1:2]
        cb_col, dtb_col, d_col, sb1_col, sb3_col = (cols[:, 2 + 2 * i:4 + 2 * i] for i in range(5))
        b1_col = cols[:, 12:VECS]
        w_in = sb("w_in", [128, 2 * E])
        w_conv = sb("w_conv", [128, TAPS, E])
        xp_in = sb("xp_in", [128, HALF, R + 2 * N])
        w_xp = sb("w_xp", [128, HALF, ROWS])
        w_dt = sb("w_dt", [ROWS, E])
        a_log, a_exp, a_neg = sb("a_log", [128, HALF, N]), sb("a_exp", [128, HALF, N]), sb("a_neg", [128, HALF, N])
        w_out = sb("w_out", [128, HALF, D])
        rs_col = sb("rs_col", [128, 1])
        w_s1, w_s3, w_s2 = sb("w_s1", [128, HID]), sb("w_s3", [128, HID]), sb("w_s2", [128, HALF, D])
        w_e1, w_e2h = sb("w_e1", [128, EXPERTS, 128]), sb("w_e2h", [128, EXPERTS, 128])
        bias_rows, route_sb = sb("bias_rows", [EXPERTS + 1, D]), sb("route_sb", [EXPERTS + 1, CH, 128])
        bias_tok = sb("bias_tok", [128, CH, D])
        minus_one = sb("minus_one", [128, 1])
        k_mhalf, k_one, k_mone = (sb(n, [128, SEQS, CH]) for n in ("k_mhalf", "k_one", "k_mone"))

        xin = sb("xin", [128, SEQS, CH, D])
        stat1, stat2 = sb("stat1", [128, SEQS, CH, 6]), sb("stat2", [128, SEQS, CH, 6])
        mv1, mv2 = sb("mv1", [128, SEQS, CH, 2]), sb("mv2", [128, SEQS, CH, 2])
        both, inv1, scale_r, shift_r, inv2 = (
            sb(n, [128, SEQS, CH]) for n in ("both", "inv1", "scale_r", "shift_r", "inv2"))
        xnT = sb("xnT", [128, SEQS, KEEP])
        u2, gz = sb("u2", [128, 2, HALF, T]), sb("gz", [128, 2, HALF, T])
        small = sb("small", [ROWS, 2, T])
        bexp, brelu, bln, bcor = (sb(n, [128, HALF, T]) for n in ("bexp", "brelu", "bln", "bcor"))
        dt, wdt = sb("dt", [128, 2, HALF, T]), sb("wdt", [128, 2, HALF, T])
        bcbc = sb("bcbc", [128, RING * STATES, 2, T])
        decay = sb("decay", [128, DECAYS, T])
        drive = sb("drive", [128, DRIVES, HALF, T])
        h = sb("h", [128, 2, HALF, T])
        hc = sb("hc", [128, HCS, HALF, T])
        xn = hc[:, 0:2].rearrange("p r h t -> p (r h t)").rearrange("p (b c d) -> p b c d", b=SEQS, c=CH)
        yd, yg = sb("yd", [128, HALF, T]), sb("yg", [128, HALF, T])
        taps = yd[:, :, :].rearrange("p h t -> p (h t)").rearrange("p (e k) -> p e k", k=TAPS)
        w_e2 = yg[:, :, :].rearrange("p h t -> p (h t)").rearrange("p (e c) -> p e c", e=EXPERTS)
        x1, x1b = sb("x1", [128, CH, D]), sb("x1b", [128, CH, D])
        xn2, xT = sb("xn2", [128, CH, D]), sb("xT", [128, T])
        hs1, hs = sb("hs1", [128, HALF, T]), yd
        he = sb("he", [128, EXPERTS, 2 * CLASS])
        fo = hs1[:, 0]
        res = sb("res", [128, 2, CH, D])

        yacc = [ps(f"yacc{i}", [128, HALF, T]) for i in range(2)]
        bank = [ps(f"bank{i}", [128, T]) for i in range(BANKS)]
        early = [yacc[0][:, 0, :], yacc[1][:, 0, :], yacc[1][:, 1, :]]

        x_in = [sem(f"x_in{b}") for b in range(SEQS)]
        in_vecs, in_vecs2, in_w_in, in_w_mid, in_w_scan, in_w_ffn = (
            sem(n) for n in ("in_vecs", "in_vecs2", "in_w_in", "in_w_mid", "in_w_scan", "in_w_ffn"))
        const_ok, pad_ok, conv_ok, xpw_ok = (sem(n) for n in ("const_ok", "pad_ok", "conv_ok", "xpw_ok"))
        a_ok, aneg_ok, e2h_ok, bias_ok, cols_ok = (sem(n) for n in ("a_ok", "aneg_ok", "e2h_ok", "bias_ok", "cols_ok"))
        cols2_ok, early_ok = sem("cols2_ok"), sem("early_ok")
        stat1_ok, mv1_ok, fac1_ok, facr_ok, stat2_ok, mv2_ok, fac2_ok, var1_ok, var2_ok, one_ok = (
            sem(n) for n in ("stat1_ok", "mv1_ok", "fac1_ok", "facr_ok", "stat2_ok", "mv2_ok", "fac2_ok", "var1_ok",
                             "var2_ok", "one_ok"))
        pool_chain = sem("pool_chain")
        xn_ok, xres_ok, xnT_ok, u2_ok = (sem(n) for n in ("xn_ok", "xres_ok", "xnT_ok", "u2_ok"))
        small_ok, bc_out = sem("small_ok"), sem("bc_out")
        bcbc_in = [sem(f"bcbc_in{i}") for i in range(RING)]
        babs_ok, brelu_ok, bexp_ok, bln_ok = (sem(n) for n in ("babs_ok", "brelu_ok", "bexp_ok", "bln_ok"))
        bcor_ok, bcor2_ok, bsum_ok, dt_ok, wdt_ok = (sem(n) for n in ("bcor_ok", "bcor2_ok", "bsum_ok", "dt_ok", "wdt_ok"))
        filled = sem("filled")
        freed = [sem(f"freed{i}") for i in range(BANKS)]
        decay_ok, drive_ok, scan_ok, hc_ok, yacc_ok = (
            sem(n) for n in ("decay_ok", "drive_ok", "scan_ok", "hc_ok", "yacc_ok"))
        yd_ok, yg_ok, x1_ok, x1b_ok, xn2_ok, xT_ok = (sem(n) for n in ("yd_ok", "yg_ok", "x1_ok", "x1b_ok", "xn2_ok", "xT_ok"))
        hs1_ok, hs_ok, he_ok, fo_ok, res_ok = (sem(n) for n in ("hs1_ok", "hs_ok", "he_ok", "fo_ok", "res_ok"))
        stored = sem("stored")

        def tokens(v):
            return v.rearrange("(i c jj) d -> jj i c d", c=CH, jj=2)

        def softplus_end(eng, on, s, b, hfs=slice(0, HALF)):
            halves, done = hfs.stop - hfs.start, 2 * b + hfs.stop
            if s == "cor":
                eng.wait_ge(one_ok, b)
                on.tensor_tensor(out=bcor[:, hfs, :], in0=bexp[:, hfs, :], in1=bcor[:, hfs, :],
                                 op=ALU.subtract).then_inc(bcor2_ok, halves)
            elif s == "sum":
                eng.wait_ge(bcor2_ok, done)
                eng.wait_ge(brelu_ok, done)
                on.tensor_tensor(out=brelu[:, hfs, :], in0=brelu[:, hfs, :], in1=bcor[:, hfs, :],
                                 op=ALU.add).then_inc(bsum_ok, halves)
            elif s == "dt":
                eng.wait_ge(bln_ok, done)
                eng.wait_ge(bsum_ok, done)
                on.tensor_tensor(out=dt[:, b % 2, hfs], in0=bln[:, hfs, :], in1=brelu[:, hfs, :],
                                 op=ALU.add).then_inc(dt_ok, halves)
            else:
                eng.wait_ge(dt_ok, done)
                if b == 0:
                    eng.wait_ge(u2_ok, 2)
                on.tensor_tensor(out=wdt[:, b % 2, hfs], in0=dt[:, b % 2, hfs], in1=u2[:, b % 2, hfs],
                                 op=ALU.mult).then_inc(wdt_ok, halves)

        def y_of(b):
            return yd if b < SEQS - 1 else brelu

        def gate(eng, on, b, hfs=slice(0, HALF)):
            eng.wait_ge(yd_ok, 2 * b + hfs.stop)
            if b == 0:
                eng.wait_ge(e2h_ok, 1)
            if b >= 1:
                eng.wait_ge(x1_ok, b)
            on.tensor_tensor(out=yg[:, hfs, :], in0=y_of(b)[:, hfs, :], in1=gz[:, b % 2, hfs],
                             op=ALU.mult).then_inc(yg_ok, hfs.stop - hfs.start)

        def store(eng, b, jj):
            eng.dma_start(tokens(out[b])[jj], res[64 * jj:64 * jj + 64, b % 2]).then_inc(stored, 16)

        def drives(g):
            return g + 2

        block = ctx.enter_context(nc.Block())

        @block.sync
        def _(sp):
            for b in range(SEQS):
                for jj in range(2):
                    sp.dma_start(xin[64 * jj:64 * jj + 64, b], tokens(x[b])[jj]).then_inc(x_in[b], 16)
                if b == 0:
                    sp.dma_start(w_in[:, :], W_in).then_inc(in_w_in, 16)
                    sp.dma_start(taps.rearrange("p e k -> p (e k)"),
                                 conv_w.rearrange("e k -> (e k)").partition_broadcast(128)).then_inc(in_w_in, 16)
            for i, vec in enumerate((D_param, sb1, sb3, b1)):
                src = vec if len(vec.shape) == 2 else vec.rearrange("(h p) -> h p", p=128)
                sp.dma_start(vec_rows2[2 * i:2 * i + src.shape[0], :], src).then_inc(in_vecs2, 16)
            sp.dma_start(bias_rows[0:EXPERTS, :], b2).then_inc(in_w_ffn, 16)
            sp.dma_start(bias_rows[EXPERTS:EXPERTS + 1, :], sb2.rearrange("(o d) -> o d", o=1)).then_inc(in_w_ffn, 16)
            sp.dma_start(route_sb[:, :, :], route).then_inc(in_w_ffn, 16)
            sp.dma_start(w_out[:, :, :], W_out.rearrange("(h p) d -> p h d", p=128)).then_inc(in_w_ffn, 16)
            sp.dma_start(w_s1[:, :], sw1).then_inc(in_w_ffn, 16)
            sp.dma_start(w_s3[:, :], sw3).then_inc(in_w_ffn, 16)
            sp.dma_start(w_s2[:, :, :], sw2.rearrange("(h p) d -> p h d", p=128)).then_inc(in_w_ffn, 16)
            sp.dma_start(w_e1[:, :, :], w1.rearrange("e c h -> c e h")).then_inc(in_w_ffn, 16)
            sp.dma_start(w_e2, w2.rearrange("e h c -> h e c")).then_inc(in_w_ffn, 16)
            sp.dma_start(rs_col[:, :], res_scale.partition_broadcast(128)).then_inc(in_w_ffn, 16)

            def load_bc(g):
                b, n = divmod(g, N)
                if g >= RING * STATES:
                    sp.wait_ge(drive_ok, drives(g + STATES - RING * STATES - 1))
                    sp.wait_ge(hc_ok, g + STATES - RING * STATES)
                at = g % (RING * STATES)
                sp.dma_start(bcbc[:, at:at + STATES].rearrange("p n k t -> p (n k t)"),
                             bc_scratch[b, n:n + STATES].rearrange("n k t -> (n k t)").partition_broadcast(128))\
                  .then_inc(bcbc_in[g // STATES % RING], 16)

            for item in order("SP"):
                if item[0] == "unit":
                    g = N * item[1] + item[2] + AHEAD
                    if g % STATES == 0 and g < N * SEQS:
                        load_bc(g)
                if item[0] == "bc_out":
                    b = item[1]
                    sp.wait_ge(small_ok, b + 1)
                    sp.dma_start(bc_scratch[b].rearrange("n k t -> (n k) t"), small[0:ROW_DT, b % 2, :]).then_inc(bc_out, 16)
                    sp.wait_ge(bc_out, 16 * (b + 1))
                    if b == 0:
                        for g in range(0, AHEAD, STATES):
                            load_bc(g)
                if item[0] == "store":
                    b = item[1]
                    sp.wait_ge(res_ok, b + 1)
                    store(sp, b, 0)
                    if b < SEQS - 1:
                        store(sp, b, 1)
            sp.wait_ge(stored, 32 * SEQS)

        @block.gpsimd
        def _(pool):
            chain, tt = [0], nc.gpsimd.tensor_tensor

            def link(ins):
                chain[0] += 1
                ins.then_inc(pool_chain, 1)
                pool.wait_ge(pool_chain, chain[0])

            pool.dma_start(xp_in[:, :, :], W_xp.rearrange("(h p) r -> p h r", p=128)).then_inc(in_w_mid, 16)
            pool.dma_start(w_dt[ROW_DT:ROWS, :], W_dt).then_inc(in_w_mid, 16)
            pool.dma_start(a_log[:, :, :], A_log.rearrange("(h p) n -> p h n", p=128)).then_inc(in_w_scan, 16)

            nc.gpsimd.memset(k_mhalf[:, :, :], -0.5)
            nc.gpsimd.memset(k_one[:, :, :], 1.0)
            nc.gpsimd.memset(k_mone[:, :, :], -1.0)
            nc.gpsimd.memset(minus_one[:, :], -1.0)
            link(nc.gpsimd.memset(ident[:, :], 0.0))
            nc.gpsimd.affine_select(out=ident[:, :], in_=ident[:, :], compare_op=ALU.not_equal, fill=1.0, base=0,
                                    pattern=[[-1, 128]], channel_multiplier=1).then_inc(const_ok, 1)
            nc.gpsimd.memset(xnT[:, :, 0:TAPS - 1], 0.0).then_inc(pad_ok, 1)

            def unit(g):
                b, n = divmod(g, N)
                if n == 0:
                    pool.wait_ge(wdt_ok, 2 * (b + 1))
                if g % STATES == 0:
                    pool.wait_ge(bcbc_in[g // STATES % RING], 16 * (g // STATES // RING + 1))
                if g >= DRIVES:
                    pool.wait_ge(scan_ok, 2 * (g - DRIVES + 1))
                nc.gpsimd.tensor_tensor(out=drive[:, g % DRIVES], in0=wdt[:, b % 2],
                                        in1=bcbc[:, g % (RING * STATES), 0, :].unsqueeze(1).broadcast_to([128, HALF, T]),
                                        op=ALU.mult).then_inc(drive_ok, 1)

            for item in order("POOL"):
                s, b = item[0], item[1]
                if s == "unit":
                    g = N * b + item[2]
                    if g == 0:
                        pool.wait_ge(bcbc_in[0], 16)
                        for hf in range(HALF):
                            pool.wait_ge(wdt_ok, hf + 1)
                            nc.gpsimd.tensor_tensor(out=drive[:, 0, hf], in0=wdt[:, 0, hf], in1=bcbc[:, 0, 0, :],
                                                    op=ALU.mult).then_inc(drive_ok, 1)
                        for ahead in range(1, LEAD):
                            unit(ahead)
                    if g + LEAD < N * SEQS:
                        unit(g + LEAD)
                elif s == "fac1":
                    seqs = slice(0, 1) if b == 0 else slice(1, SEQS)
                    pool.wait_ge(var1_ok, 2 * seqs.stop)
                    tt(out=both[:, seqs, :], in0=both[:, seqs, :], in1=k_mhalf[:, seqs, :], op=ALU.pow).then_inc(fac1_ok, 1)
                elif s == "facr":
                    link(tt(out=inv1[:, :, :], in0=inv1[:, :, :], in1=k_mhalf[:, :, :], op=ALU.pow))
                    tt(out=scale_r[:, :, :], in0=inv1[:, :, :], in1=k_one[:, :, :], op=ALU.add)
                    link(tt(out=shift_r[:, :, :], in0=inv1[:, :, :], in1=mv1[:, :, :, 0], op=ALU.mult))
                    tt(out=shift_r[:, :, :], in0=shift_r[:, :, :], in1=k_mone[:, :, :], op=ALU.mult).then_inc(facr_ok, 1)
                elif s in ("cor", "sum", "dt", "wdt"):
                    softplus_end(pool, nc.gpsimd, s, b)
                elif s == "gate":
                    gate(pool, nc.gpsimd, b)
                elif s == "fac2":
                    pool.wait_ge(var2_ok, b + 1)
                    tt(out=inv2[:, b, :], in0=inv2[:, b, :], in1=k_mhalf[:, b, :], op=ALU.pow).then_inc(fac2_ok, 1)
                elif s == "x1b":
                    if b == 0:
                        pool.wait_ge(bias_ok, 1)
                    if b >= 1:
                        pool.wait_ge(res_ok, b)
                    tt(out=x1b[:, :, :], in0=x1[:, :, :], in1=bias_tok[:, :, :], op=ALU.add).then_inc(x1b_ok, 1)

        @block.scalar
        def _(act):
            fn = nc.scalar.activation
            for i, vec in enumerate((ln_g, ln_b, conv_b, b_dt)):
                row = i if i < 2 else 2 * i - 2
                src = vec.rearrange("(h p) -> h p", p=128)
                act.dma_start(vec_rows[row:row + src.shape[0], :], src).then_inc(in_vecs, 16)

            def full(step, b):
                u = USES[step, b]
                act.wait_ge(filled, FILLED[step, b] + 1)
                return bank[u % BANKS], u % BANKS

            def log_exp():
                nc.scalar.preload_act_table_set("natural_log_exp_and_others")

            def decays(g):
                b, n = divmod(g, N)
                for hf in range(HALF):
                    r = 2 * g + hf
                    if n == 0:
                        act.wait_ge(dt_ok, 2 * b + hf + 1)
                    if r >= DECAYS:
                        act.wait_ge(scan_ok, r - DECAYS + 1)
                    fn(decay[:, r % DECAYS, :], dt[:, b % 2, hf, :], ACT.Exp,
                       scale=a_neg[:, hf, n:n + 1]).then_inc(decay_ok, 1)

            def silu_u(hf, b):
                m, k = full(f"u{hf}", b)
                if b >= 2:
                    act.wait_ge(yd_ok, 2 * (b - 1))
                fn(u2[:, b % 2, hf], m[:, :], ACT.Silu, bias=cb_col[:, hf:hf + 1]).then_inc(u2_ok, 1)
                act.wait_ge(u2_ok, 2 * b + hf + 1)
                act.sem_inc(freed[k], 1)

            def silu_z(hf, b):
                m, k = full(f"z{hf}", b)
                if b >= 2:
                    act.wait_ge(yg_ok, 2 * (b - 1))
                fn(gz[:, b % 2, hf].rearrange("p (j i) -> p j i", j=8),
                   m[:, :].rearrange("p (i j) -> p j i", j=8), ACT.Silu).then_inc(freed[k], 1)

            for item in order("ACT"):
                s, b = item[0], item[1]
                if s == "unit":
                    g = N * b + item[2]
                    if g == 0:
                        act.wait_ge(aneg_ok, 1)
                        for ahead in range(LEAD):
                            decays(ahead)
                    if g + LEAD < N * SEQS:
                        decays(g + LEAD)
                elif s == "silu":
                    nc.scalar.preload_act_table_set("silu_and_others")
                elif s == "store":
                    act.wait_ge(res_ok, b + 1)
                    store(act, b, 1)
                elif s == "gelu":
                    nc.scalar.preload_act_table_set("gelu_and_others")
                elif s == "cols":
                    m, k = full(s, b)
                    fn(cols[:, 0:VECS1], m[:, 0:VECS1], ACT.Identity).then_inc(cols_ok, 1)
                    act.wait_ge(cols_ok, 1)
                    act.sem_inc(freed[k], 1)
                elif s == "a_exp":
                    act.wait_ge(in_w_scan, 16)
                    fn(a_exp[:, :, :], a_log[:, :, :], ACT.Exp).then_inc(a_ok, 1)
                elif s == "one":
                    act.wait_ge(bsum_ok, 2 * b)
                    fn(bcor[:, :, :], bexp[:, :, :], ACT.Identity, bias=1.0).then_inc(bcor_ok, 2)
                    act.wait_ge(bcor_ok, 2 * (b + 1))
                    fn(bcor[:, :, :], bcor[:, :, :], ACT.Identity, bias=minus_one[:, :]).then_inc(one_ok, 1)
                elif s == "tr1":
                    if b == 0:
                        m, k = full("tr1", b)
                    else:
                        act.wait_ge(early_ok, b)
                        m = early[b - 1]
                        act.wait_ge(xnT_ok, b)
                    fn(xnT[:, b, TAPS - 1:].rearrange("p (i j) -> p j i", j=8),
                       m[:, :].rearrange("p (j i) -> p j i", j=8), ACT.Identity,
                       scale=g_col, bias=b_col).then_inc(xnT_ok, 1)
                    if b == 0:
                        act.wait_ge(xnT_ok, 1)
                        act.sem_inc(freed[k], 1)
                elif s == "xres":
                    act.wait_ge(facr_ok, 1)
                    act.wait_ge(xn_ok, b + 1)
                    for c in range(CH):
                        fn(xin[:, b, c, :], xin[:, b, c, :], ACT.Identity, scale=scale_r[:, b, c:c + 1],
                           bias=shift_r[:, b, c:c + 1]).then_inc(xres_ok, 1)
                elif s in ("u0", "u1"):
                    silu_u(int(s[1]), b)
                elif s in ("z0", "z1"):
                    silu_z(int(s[1]), b)
                    if s == "z1":
                        log_exp()
                elif s == "uz":
                    for hf in range(HALF):
                        silu_u(hf, b)
                    for hf in range(HALF):
                        silu_z(hf, b)
                    log_exp()
                elif s == "xd":
                    m, k = full(s, b)
                    fn(small[:, b % 2], m[0:ROWS, :], ACT.Identity).then_inc(small_ok, 1)
                    act.wait_ge(small_ok, b + 1)
                    act.sem_inc(freed[k], 1)
                elif s in ("soft", "relu", "exp", "ln"):
                    for hfs in ([slice(0, 1), slice(1, 2)] if b == 0 else [slice(0, HALF)]):
                        halves, done = hfs.stop - hfs.start, 2 * b + hfs.stop
                        if s in ("soft", "relu"):
                            for hf in range(hfs.start, hfs.stop):
                                m, k = full(f"dt{hf}", b)
                                if b >= 1:
                                    act.wait_ge(bcor2_ok, 2 * b)
                                    act.wait_ge(dt_ok, 2 * b)
                                fn(bexp[:, hf], m[:, :], ACT.Abs, bias=dtb_col[:, hf:hf + 1]).then_inc(babs_ok, 1)
                                fn(brelu[:, hf], m[:, :], ACT.Relu, bias=dtb_col[:, hf:hf + 1]).then_inc(brelu_ok, 1)
                                if s == "relu":
                                    act.wait_ge(brelu_ok, 2 * b + hf + 1)
                                    act.sem_inc(freed[k], 1)
                        if s in ("soft", "exp"):
                            act.wait_ge(babs_ok, done)
                            fn(bexp[:, hfs, :], bexp[:, hfs, :], ACT.Exp, scale=-1.0).then_inc(bexp_ok, halves)
                        if s in ("soft", "ln"):
                            act.wait_ge(bexp_ok, done)
                            fn(bln[:, hfs, :], bexp[:, hfs, :], ACT.Ln, bias=1.0).then_inc(bln_ok, halves)
                        if s == "soft":
                            act.wait_ge(brelu_ok, hfs.stop)
                            act.sem_inc(freed[k], 1)
                elif s == "tr2":
                    m, k = full(s, b)
                    fn(xT[:, :], m[:, :], ACT.Identity).then_inc(xT_ok, 1)
                    act.wait_ge(xT_ok, b + 1)
                    act.sem_inc(freed[k], 1)
                elif s == "s":
                    for hf in range(HALF):
                        m, k = full(f"s{hf}", b)
                        fn(hs1[:, hf], m[:, :], ACT.Silu, bias=sb1_col[:, hf:hf + 1]).then_inc(hs1_ok, 1)
                        if hf == 1 and b < SEQS - 1:
                            log_exp()
                        act.wait_ge(hs1_ok, 2 * b + hf + 1)
                        act.sem_inc(freed[k], 1)
                elif s == "eu":
                    for part in range(2):
                        m, k = full(f"eu{part}", b)
                        for i in range(4):
                            e = 4 * part + i
                            ins = fn(he[:, e, :], m[:, i * 128:(i + 1) * 128], ACT.Gelu, bias=b1_col[:, e:e + 1])
                        ins.then_inc(he_ok, 1)
                        if part == 1 and b < SEQS - 1:
                            log_exp()
                        act.wait_ge(he_ok, 2 * b + part + 1)
                        act.sem_inc(freed[k], 1)
                elif s == "fo":
                    m, k = full(s, b)
                    fn(fo[:, :], m[:, :], ACT.Identity).then_inc(fo_ok, 1)
                    act.wait_ge(fo_ok, b + 1)
                    act.sem_inc(freed[k], 1)

        @block.tensor
        def _(pe):
            mm = nc.tensor.matmul

            def by_class(v):
                return v.rearrange("p (j i) -> p j i", j=8)

            def take(step, b):
                u = USES[step, b]
                if u >= BANKS:
                    pe.wait_ge(freed[u % BANKS], u // BANKS)
                return bank[u % BANKS]

            def accumulate(g):
                b, n = divmod(g, N)
                pe.wait_ge(hc_ok, g + 1)
                if g == N:
                    pe.wait_ge(xnT_ok, SEQS)
                if n == 0 and b >= 2:
                    pe.wait_ge(yd_ok, 2 * (b - 1))
                for hf in range(HALF):
                    if g == N * SEQS - 1:
                        pe.wait_ge(hc_ok, g + hf + 1)
                    ins = mm(yacc[b % 2][:, hf, :], ident[:, :], hc[:, g % HCS, hf], start=(n == 0), stop=(n == N - 1))
                    if g == N * SEQS - 1 or hf == HALF - 1:
                        ins.then_inc(yacc_ok, 1)

            for item in order("PE"):
                s, b = item[0], item[1]
                if s == "unit":
                    n = item[2]
                    g = N * b + n
                    if g == 0:
                        pe.wait_ge(xnT_ok, 2)
                    if n >= 1:
                        accumulate(g - 1)
                elif s == "warm":
                    pe.wait_ge(const_ok, 1)
                    for i in range(WARM):
                        mm(yacc[1][:, 0, 0:128], ident[:, :], ident[:, :], start=True, stop=True)
                elif s == "cols":
                    pe.wait_ge(in_vecs, 16 * 4)
                    nc.tensor.transpose(take(s, b)[:, 0:VECS1], vec_rows[:, :], ident[0:VECS1, 0:VECS1]).then_inc(filled, 1)
                elif s == "cols2":
                    pe.wait_ge(in_vecs2, 16 * 4)
                    rows = VECS - VECS1
                    nc.tensor.transpose(take(s, b)[:, 0:rows], vec_rows2[:, :], ident[0:rows, 0:rows]).then_inc(filled, 1)
                elif s == "bias":
                    pe.wait_ge(in_w_ffn, 16 * 10)
                    m = take(s, b)
                    for c in range(CH):
                        ins = mm(m[:, c * D:(c + 1) * D], route_sb[:, c, :], bias_rows[:, :], start=True, stop=True)
                    ins.then_inc(filled, 1)
                elif s == "tr1":
                    m = take(s, b) if b == 0 else early[b - 1]
                    pe.wait_ge(xn_ok, b + 1)
                    for c in range(CH):
                        ins = nc.tensor.transpose(m[:, c * 128:(c + 1) * 128], xn[:, b, c, :], ident[:, :])
                    ins.then_inc(filled if b == 0 else early_ok, 1)
                elif s in ("u0a", "u0b", "u1a", "u1b"):
                    hf = int(s[1])
                    m = take(s[:2], b) if s[2] == "a" else bank[USES[s[:2], b] % BANKS]
                    if s == "u0a":
                        if b == 0:
                            pe.wait_ge(pad_ok, 1)
                        pe.wait_ge(xnT_ok, b + 1)
                    for k in ((0, 1) if s[2] == "a" else (2, 3)):
                        if b == 0 and hf == 0:
                            pe.wait_ge(conv_ok, k + 1)
                        ins = mm(m[:, :], w_conv[:, k, hf * 128:(hf + 1) * 128], xnT[:, b, k:k + T],
                                 start=(k == 0), stop=(k == TAPS - 1))
                    if s[2] == "b":
                        ins.then_inc(filled, 1)
                elif s in ("z0", "z1"):
                    m = take(s, b)
                    hf = int(s[1])
                    mm(m[:, :], w_in[:, E + hf * 128:E + (hf + 1) * 128], xnT[:, b, TAPS - 1:],
                       start=True, stop=True).then_inc(filled, 1)
                elif s == "xd":
                    m = take(s, b)
                    if b == 0:
                        pe.wait_ge(xpw_ok, 3 * HALF)
                    pe.wait_ge(u2_ok, 2 * (b + 1))
                    for hf in range(HALF):
                        ins = mm(m[0:ROWS, :], w_xp[:, hf, :], u2[:, b % 2, hf], start=(hf == 0), stop=(hf == 1))
                    ins.then_inc(filled, 1)
                elif s == "dt":
                    pe.wait_ge(small_ok, b + 1)
                    for hf in range(HALF):
                        m = take(f"dt{hf}", b)
                        mm(m[:, :], w_dt[ROW_DT:ROWS, hf * 128:(hf + 1) * 128], small[ROW_DT:ROWS, b % 2],
                           start=True, stop=True).then_inc(filled, 1)
                elif s == "y":
                    accumulate(N * b + N - 1)
                elif s == "wo":
                    m = take(s, b)
                    pe.wait_ge(yg_ok, 2 * (b + 1))
                    for c in range(CH):
                        for hf in range(HALF):
                            ins = mm(m[:, c * D:(c + 1) * D], yg[:, hf, c * 128:(c + 1) * 128], w_out[:, hf, :],
                                     start=(hf == 0), stop=(hf == 1))
                    ins.then_inc(filled, 1)
                elif s == "tr2":
                    m = take(s, b)
                    pe.wait_ge(xn2_ok, CH * (b + 1))
                    for c in range(CH):
                        ins = nc.tensor.transpose(m[:, c * 128:(c + 1) * 128], xn2[:, c, :], ident[:, :])
                    ins.then_inc(filled, 1)
                elif s in ("s0", "s1", "g0", "g1"):
                    m = take(s, b)
                    hf = int(s[1])
                    pe.wait_ge(xT_ok, b + 1)
                    w = w_s1 if s[0] == "s" else w_s3
                    mm(m[:, :], w[:, hf * 128:(hf + 1) * 128], xT[:, :], start=True, stop=True).then_inc(filled, 1)
                elif s in ("eu0", "eu1"):
                    m = take(s, b)
                    for i in range(4):
                        e = 4 * int(s[2]) + i
                        ins = mm(m[:, i * 128:(i + 1) * 128].rearrange("p (k i) -> p k i", k=2), w_e1[:, e, :],
                                 by_class(xT[:, :])[:, classes_of(e), :], start=True, stop=True)
                    ins.then_inc(filled, 1)
                elif s == "fo0":
                    m = take("fo", b)
                    for hf in range(HALF):
                        pe.wait_ge(hs_ok, 2 * b + hf + 1)
                        mm(m[:, :], w_s2[:, hf, :], hs[:, hf], start=(hf == 0), stop=False)
                elif s in ("fo1", "fo2"):
                    m = bank[USES["fo", b] % BANKS]
                    part = int(s[2])
                    pe.wait_ge(he_ok, 2 * b + part)
                    if b == 0:
                        pe.wait_ge(e2h_ok, 1)
                    for e in range(4 * part - 4, 4 * part):
                        ins = mm(by_class(m[:, :])[:, classes_of(e), :], w_e2h[:, e, :],
                                 he[:, e, :].rearrange("p (k i) -> p k i", k=2), start=False, stop=(e == EXPERTS - 1))
                    if s == "fo2":
                        ins.then_inc(filled, 1)
                elif s == "bt":
                    m = take(s, b)
                    pe.wait_ge(fo_ok, b + 1)
                    for c in range(CH):
                        ins = nc.tensor.transpose(m[:, c * 128:(c + 1) * 128], fo[:, c * 128:(c + 1) * 128], ident[:, :])
                    ins.then_inc(filled, 1)

        @block.vector
        def _(dve):
            v = nc.vector

            def full(step, b):
                u = USES[step, b]
                dve.wait_ge(filled, FILLED[step, b] + 1)
                return bank[u % BANKS], u % BANKS

            def stats(src, stat, mv, stat_ok, mv_ok, b):
                for c in range(CH):
                    v.bn_stats(out=stat[:, b, c, :], in_=src[:, c, :]).then_inc(stat_ok, 1)
                for c in range(CH):
                    dve.wait_ge(stat_ok, CH * b + c + 1)
                    v.bn_aggr(out=mv[:, b, c, :], in_=stat[:, b, c, :]).then_inc(mv_ok, 1)
                dve.wait_ge(mv_ok, CH * (b + 1))

            def correction(b, hfs=slice(0, HALF)):
                halves, done = hfs.stop - hfs.start, 2 * b + hfs.stop
                dve.wait_ge(bexp_ok, done)
                v.tensor_scalar(bcor[:, hfs, :], bexp[:, hfs, :], 1.0, 1.0, ALU.add, ALU.subtract).then_inc(bcor_ok, halves)
                dve.wait_ge(bcor_ok, done)
                v.tensor_tensor(out=bcor[:, hfs, :], in0=bexp[:, hfs, :], in1=bcor[:, hfs, :],
                                op=ALU.subtract).then_inc(bcor2_ok, halves)

            for item in order("DVE"):
                s, b = item[0], item[1]
                if s == "unit":
                    n = item[2]
                    g = N * b + n
                    if g > 0:
                        dve.wait_ge(drive_ok, drives(g))
                    for hf in range(HALF):
                        r = 2 * g + hf
                        dve.wait_ge(decay_ok, r + 1)
                        if g == 0:
                            dve.wait_ge(drive_ok, hf + 1)
                        v.tensor_tensor_scan(h[:, g % 2, hf, :], decay[:, r % DECAYS, :], drive[:, g % DRIVES, hf], 0.0,
                                             ALU.mult, ALU.add).then_inc(scan_ok, 1)
                    dve.wait_ge(scan_ok, 2 * g + 2)
                    if g % STATES == 0:
                        dve.wait_ge(bcbc_in[g // STATES % RING], 16 * (g // STATES // RING + 1))
                    if g == 0:
                        dve.wait_ge(early_ok, SEQS - 1)
                    if g >= HCS:
                        dve.wait_ge(yacc_ok, g - HCS + 1)
                    c_row = bcbc[:, g % (RING * STATES), 1, :]
                    if g == N * SEQS - 1:
                        for hf in range(HALF):
                            v.tensor_tensor(out=hc[:, g % HCS, hf], in0=h[:, g % 2, hf], in1=c_row,
                                            op=ALU.mult).then_inc(hc_ok, 1)
                    else:
                        v.tensor_tensor(out=hc[:, g % HCS], in0=h[:, g % 2],
                                        in1=c_row.unsqueeze(1).broadcast_to([128, HALF, T]), op=ALU.mult).then_inc(hc_ok, 1)
                elif s == "ln1":
                    dve.wait_ge(x_in[b], 32)
                    stats(xin[:, b], stat1, mv1, stat1_ok, mv1_ok, b)
                    v.tensor_scalar(both[:, b, :], mv1[:, b, :, 1], 1.0 + EPS, EPS * EPS, ALU.mult, ALU.add).then_inc(var1_ok, 1)
                    v.tensor_scalar(inv1[:, b, :], mv1[:, b, :, 1], EPS, None, ALU.add).then_inc(var1_ok, 1)
                elif s == "w_conv":
                    dve.wait_ge(in_w_in, 32)
                    for k in range(TAPS):
                        v.tensor_tensor(out=w_conv[:, k, :], in0=w_in[:, 0:E], in1=taps[:, :, k],
                                        op=ALU.mult).then_inc(conv_ok, 1)
                elif s == "w_xp":
                    dve.wait_ge(in_w_mid, 32)
                    for hf in range(HALF):
                        rows = w_xp[:, hf, 0:ROW_DT].rearrange("p (n k) -> p n k", k=2)
                        v.tensor_copy(rows[:, :, 0], xp_in[:, hf, R:R + N]).then_inc(xpw_ok, 1)
                        v.tensor_copy(rows[:, :, 1], xp_in[:, hf, R + N:R + 2 * N]).then_inc(xpw_ok, 1)
                        v.tensor_copy(w_xp[:, hf, ROW_DT:ROWS], xp_in[:, hf, 0:R]).then_inc(xpw_ok, 1)
                elif s == "a_neg":
                    dve.wait_ge(a_ok, 1)
                    v.tensor_scalar(a_neg[:, :, :], a_exp[:, :, :], -1.0, None, ALU.mult).then_inc(aneg_ok, 1)
                elif s == "cols2":
                    m, k = full(s, b)
                    v.tensor_copy(cols[:, VECS1:VECS], m[:, 0:VECS - VECS1]).then_inc(cols2_ok, 1)
                    dve.wait_ge(cols2_ok, 1)
                    dve.sem_inc(freed[k], 1)
                elif s == "xn":
                    dve.wait_ge(fac1_ok, min(b, 1) + 1)
                    for c in range(CH):
                        ins = v.tensor_scalar(xn[:, b, c, :], xin[:, b, c, :], mv1[:, b, c, 0:1], both[:, b, c:c + 1],
                                              ALU.subtract, ALU.mult)
                    ins.then_inc(xn_ok, 1)
                elif s == "tr1":
                    dve.wait_ge(cols_ok, 1)
                    dve.wait_ge(early_ok, b)
                    v.tensor_scalar(xnT[:, b, TAPS - 1:].rearrange("p (i j) -> p j i", j=8),
                                    early[b - 1].rearrange("p (j i) -> p j i", j=8), g_col, b_col,
                                    ALU.mult, ALU.add).then_inc(xnT_ok, 1)
                elif s == "xn2":
                    dve.wait_ge(fac2_ok, b + 1)
                    if b >= 1:
                        dve.wait_ge(xT_ok, b)
                    for c in range(CH):
                        v.tensor_scalar(xn2[:, c, :], x1[:, c, :], mv2[:, b, c, 0:1], inv2[:, b, c:c + 1],
                                        ALU.subtract, ALU.mult).then_inc(xn2_ok, 1)
                elif s == "bias":
                    m, k = full(s, b)
                    v.tensor_copy(bias_tok[:, :, :].rearrange("p c d -> p (c d)"), m[:, :]).then_inc(bias_ok, 1)
                    dve.wait_ge(bias_ok, 1)
                    dve.sem_inc(freed[k], 1)
                    v.tensor_scalar(w_e2h[:, :, :], w_e2, 0.5, None, ALU.mult).then_inc(e2h_ok, 1)
                elif s == "soft":
                    for hf in range(HALF):
                        correction(b, slice(hf, hf + 1))
                        for step in ("sum", "dt", "wdt"):
                            softplus_end(dve, v, step, b, slice(hf, hf + 1))
                elif s == "y":
                    if b >= 1:
                        dve.wait_ge(yg_ok, 2 * b)
                    for hf in range(HALF):
                        dve.wait_ge(yacc_ok, N * (b + 1) + (hf if b == SEQS - 1 else 0))
                        v.scalar_tensor_tensor(out=y_of(b)[:, hf].rearrange("p (j i) -> p j i", j=8),
                                               in0=u2[:, b % 2, hf].rearrange("p (i j) -> p j i", j=8),
                                               scalar=d_col[:, hf:hf + 1],
                                               in1=yacc[b % 2][:, hf, :].rearrange("p (i j) -> p j i", j=8),
                                               op0=ALU.mult, op1=ALU.add).then_inc(yd_ok, 1)
                        if b == SEQS - 1:
                            gate(dve, v, b, slice(hf, hf + 1))
                elif s == "wo":
                    m, k = full(s, b)
                    dve.wait_ge(xres_ok, CH * (b + 1))
                    if b >= 1:
                        dve.wait_ge(xn2_ok, CH * b)
                        dve.wait_ge(x1b_ok, b)
                    v.scalar_tensor_tensor(out=x1[:, :, :].rearrange("p c d -> p (c d)"), in0=m[:, :], scalar=rs_col[:, :],
                                           in1=xin[:, b].rearrange("p c d -> p (c d)"),
                                           op0=ALU.mult, op1=ALU.add).then_inc(x1_ok, 1)
                    dve.wait_ge(x1_ok, b + 1)
                    dve.sem_inc(freed[k], 1)
                elif s == "ln2":
                    stats(x1, stat2, mv2, stat2_ok, mv2_ok, b)
                    v.tensor_scalar(inv2[:, b, :], mv2[:, b, :, 1], EPS, None, ALU.add).then_inc(var2_ok, 1)
                elif s in ("g0", "g1"):
                    m, k = full(s, b)
                    hf = int(s[1])
                    dve.wait_ge(hs1_ok, 2 * b + hf + 1)
                    v.scalar_tensor_tensor(out=hs[:, hf], in0=m[:, :], scalar=sb3_col[:, hf:hf + 1], in1=hs1[:, hf],
                                           op0=ALU.add, op1=ALU.mult).then_inc(hs_ok, 1)
                    dve.wait_ge(hs_ok, 2 * b + hf + 1)
                    dve.sem_inc(freed[k], 1)
                elif s == "bt":
                    m, k = full(s, b)
                    dve.wait_ge(x1b_ok, b + 1)
                    if b >= 2:
                        dve.wait_ge(stored, 32 * (b - 1))
                    v.scalar_tensor_tensor(out=res[:, b % 2].rearrange("p c d -> p (c d)"), in0=m[:, :], scalar=0.5,
                                           in1=x1b[:, :, :].rearrange("p c d -> p (c d)"),
                                           op0=ALU.mult, op1=ALU.add).then_inc(res_ok, 1)
                    dve.wait_ge(res_ok, b + 1)
                    dve.sem_inc(freed[k], 1)


_INS = ['L0_attn_x', 'L0_attn_ln_g', 'L0_attn_ln_b', 'L0_attn_W_in', 'L0_attn_conv_w', 'L0_attn_conv_b',
        'L0_attn_W_xp', 'L0_attn_W_dt', 'L0_attn_b_dt', 'L0_attn_A_log', 'L0_attn_D_param', 'L0_attn_W_out',
        'L0_attn_res_scale', 'L0_ffn_sw1', 'L0_ffn_sb1', 'L0_ffn_sw3', 'L0_ffn_sb3', 'L0_ffn_sw2', 'L0_ffn_sb2',
        'L0_ffn_w1', 'L0_ffn_b1', 'L0_ffn_w2', 'L0_ffn_b2']


def kernel(**inputs):
    import numpy as _np
    import concourse.bacc as _bacc
    from concourse import mybir as _mybir
    from concourse.bass_utils import run_bass_kernel_spmd as _run

    nc = _bacc.Bacc("TRN2", target_bir_lowering=False, num_devices=1)
    arrays, args = {}, []
    for name in _INS:
        a = _np.ascontiguousarray(inputs[name])
        arrays[f"in_{name}_dram"] = a
        args.append(nc.dram_tensor(f"in_{name}_dram", a.shape, _mybir.dt.from_np(a.dtype), kind="ExternalInput").ap())
    route = _np.zeros((EXPERTS + 1, CH, 128), _np.float32)
    for j in range(8):
        at = slice(64 * (j % 2), 64 * (j % 2) + 64)
        for e in experts_of(j):
            route[e, j // 2, at] = 0.25
        route[EXPERTS, j // 2, at] = 0.5
    arrays["route_dram"] = route
    args.append(nc.dram_tensor("route_dram", route.shape, _mybir.dt.float32, kind="ExternalInput").ap())
    args.append(nc.dram_tensor("out_0_dram", (SEQS, T, D), _mybir.dt.float32, kind="ExternalOutput").ap())
    build(nc, *args)
    r = _run(nc, [arrays], core_ids=[0])
    return r.results[0]["out_0_dram"]
```
